# Optimizing a Trainium2 kernel written in Bass

```python
import numpy as np
import jax
import jax.numpy as jnp

def _softmax(x, axis=-1):
    return jax.nn.softmax(x, axis=axis)

def _gelu(x):
    return jax.nn.gelu(x, approximate=True)

def _silu(x):
    return jax.nn.silu(x)

def _sigmoid(x):
    return jax.nn.sigmoid(x)

def _layernorm(x, axis=-1, eps=1e-05):
    m = jnp.mean(x, axis=axis, keepdims=True)
    v = jnp.var(x, axis=axis, keepdims=True)
    return (x - m) / jnp.sqrt(v + eps)

def _scatter_add(tgt, idx, src, axis=0):
    return tgt.at[idx].add(src)

def _segment_sum(src, seg, n):
    return jax.ops.segment_sum(src, seg, n)
kernel_name = 'mk_adaln_ffn_d1_seqx_r2_033c92'

def setup_inputs(seed: int=0):
    np.random.seed(seed)
    _w = jnp.asarray

    def _rec_inputs():
        import jax
        import jax.numpy as jnp
        _rk = jax.random.key(seed)
        x = -0.000125 + 0.9999 * jax.random.normal(jax.random.fold_in(_rk, 1), (32, 128, 2048), jnp.float32)
        _lenS = 128 - jax.random.randint(jax.random.fold_in(_rk, 7), (32,), 0, max(1, 128 // 4) + 1, jnp.int32)
        _lenS2 = 128 - jax.random.randint(jax.random.fold_in(_rk, 8), (32,), 0, max(1, 128 // 4) + 1, jnp.int32)
        condB_codebook = -0.0625 + 0.715345 * jax.random.normal(jax.random.fold_in(_rk, 11), (32,), jnp.float32)
        return (x, condB_codebook)
    x, condB_codebook = _rec_inputs()

    def _L0_cond_setup():
        import jax, jax.numpy as jnp
        import numpy as np
        GROUP = 128
        LORA_ALPHA = 32.0
        LORA_RANK = 64
        key = jax.random.key(seed)
        k1, k2, k3, k4 = jax.random.split(key, 4)
        O, I = (2048, 2048)
        x = jax.random.normal(k1, (4, 1024, I), dtype=jnp.float32)
        weight = jax.random.normal(k2, (O, I), dtype=jnp.float32) * 0.02
        wg = weight.reshape(O, I // GROUP, GROUP)
        scale_log = jnp.log(jnp.clip(jnp.max(jnp.abs(wg), axis=2, keepdims=True), 1e-05))
        codebook = jnp.array([-1.0, -0.25, 0.0, 1.0], dtype=jnp.float32)
        lora_A = jax.random.normal(k3, (LORA_RANK, I), dtype=jnp.float32) * 0.02
        lora_B = jax.random.normal(k4, (O, LORA_RANK), dtype=jnp.float32) * 0.02
        return {'x': x, 'weight': weight, 'scale_log': scale_log, 'codebook': codebook, 'lora_A': lora_A, 'lora_B': lora_B}
    _L0_cond_all = _L0_cond_setup()
    _L0_cond_in = {k: v for k, v in _L0_cond_all.items() if k in ('weight', 'scale_log', 'lora_A', 'lora_B')}
    del _L0_cond_all

    def _L0_ffn_setup():
        import jax, jax.numpy as jnp
        import numpy as np
        B, S, D, O, R, E = (4, 1024, 2048, 2048, 16, 8)
        SCALING = 32.0 / 16.0
        key = jax.random.key(seed)
        ks = jax.random.split(key, 7)
        x = jax.random.normal(ks[0], (B, S, D), dtype=jnp.float32)
        W_base = jax.random.normal(ks[1], (O, D), dtype=jnp.float32) * 0.02
        b_base = jnp.zeros((O,), dtype=jnp.float32)
        A_w = jax.random.normal(ks[2], (R, D), dtype=jnp.float32) * 0.02
        B_w = jax.random.normal(ks[3], (O, R), dtype=jnp.float32) * 0.02
        router_w = jax.random.normal(ks[4], (E, D), dtype=jnp.float32) * 0.02
        cores = jax.random.normal(ks[5], (E, R, R), dtype=jnp.float32)
        return {'x': x, 'W_base': W_base, 'b_base': b_base, 'A_w': A_w, 'B_w': B_w, 'router_w': router_w, 'cores': cores}
    _L0_ffn_all = _L0_ffn_setup()
    _L0_ffn_in = {k: v for k, v in _L0_ffn_all.items() if k in ('W_base', 'b_base', 'A_w', 'B_w', 'router_w', 'cores')}
    del _L0_ffn_all
    return {'x': x, 'condB_codebook': condB_codebook, 'L0_cond_weight': _L0_cond_in['weight'], 'L0_cond_scale_log': _L0_cond_in['scale_log'], 'L0_cond_lora_A': _L0_cond_in['lora_A'], 'L0_cond_lora_B': _L0_cond_in['lora_B'], 'L0_ffn_W_base': _L0_ffn_in['W_base'], 'L0_ffn_b_base': _L0_ffn_in['b_base'], 'L0_ffn_A_w': _L0_ffn_in['A_w'], 'L0_ffn_B_w': _L0_ffn_in['B_w'], 'L0_ffn_router_w': _L0_ffn_in['router_w'], 'L0_ffn_cores': _L0_ffn_in['cores']}

def reference(x, condB_codebook, L0_cond_weight, L0_cond_scale_log, L0_cond_lora_A, L0_cond_lora_B, L0_ffn_W_base, L0_ffn_b_base, L0_ffn_A_w, L0_ffn_B_w, L0_ffn_router_w, L0_ffn_cores):
    import jax
    import jax.numpy as jnp

    def _L0_cond_ref(x, weight, scale_log, codebook, lora_A, lora_B):
        import jax, jax.numpy as jnp
        import numpy as np
        GROUP = 128
        LORA_ALPHA = 32.0
        LORA_RANK = 64
        O, I = weight.shape
        lora_delta = lora_B @ lora_A * (LORA_ALPHA / LORA_RANK)
        cb = codebook / jnp.clip(jnp.max(jnp.abs(codebook)), 1e-08)
        scale = jnp.exp(scale_log)
        wg = (weight + lora_delta).reshape(O, I // GROUP, GROUP)
        normalized = wg / scale
        thresholds = (cb[:-1] + cb[1:]) * 0.5
        idx = jnp.searchsorted(thresholds, normalized, side='left')
        quantized = cb[idx]
        w = jax.lax.stop_gradient(quantized - normalized) + normalized
        w_q = (w * scale).reshape(O, I)
        w_eff = w_q + lora_delta
        return x @ w_eff.T

    def _L0_ffn_ref(x, W_base, b_base, A_w, B_w, router_w, cores):
        import jax, jax.numpy as jnp
        import numpy as np
        B, S, D, O, R, E = (4, 1024, 2048, 2048, 16, 8)
        SCALING = 32.0 / 16.0
        result = jnp.einsum('bsd,od->bso', x, W_base) + b_base
        ax = jnp.einsum('bsd,rd->bsr', x, A_w)
        probs = jax.nn.softmax(jnp.einsum('bsd,ed->bse', x, router_w), axis=-1)
        per_expert = jnp.einsum('bsr,erq->bseq', ax, cores)
        mixed = jnp.einsum('bseq,bse->bsq', per_expert, probs)
        result = result + jnp.einsum('bsr,or->bso', mixed, B_w) * SCALING
        return result
    x = x + _L0_ffn_ref(_L0_cond_ref(x, L0_cond_weight, L0_cond_scale_log, condB_codebook, L0_cond_lora_A, L0_cond_lora_B), L0_ffn_W_base, L0_ffn_b_base, L0_ffn_A_w, L0_ffn_B_w, L0_ffn_router_w, L0_ffn_cores)
    return x

_drawn_inputs = setup_inputs


def setup_inputs(seed=0):
    import zlib

    import numpy as np

    out = dict(_drawn_inputs(seed))
    spreads = {'L0_ffn_b_base': (0.0, 0.1)}
    factors = {}
    for name, (base, spread) in spreads.items():
        noise = np.random.default_rng([zlib.crc32(name.encode()), seed]).standard_normal(out[name].shape)
        drawn = base * np.exp(spread * noise) if base else spread * noise
        out[name] = jnp.asarray(drawn.astype(out[name].dtype))
    for name, factor in factors.items():
        out[name] = (out[name] * factor).astype(out[name].dtype)
    return out
```

```python
import numpy as np
from contextlib import ExitStack

import concourse.bass as bass
import concourse.mybir as mybir

F32 = mybir.dt.float32
F32R = mybir.dt.float32r
I32 = mybir.dt.int32
U8 = mybir.dt.uint8
ALU = mybir.AluOpType
ACT = mybir.ActivationFunctionType
AXX = mybir.AxisListType.X

D = 2048
NB = 16
NT = 32
NE = 8
NR = 16
XW = NE + NR
DX = D + XW
NC = 32
NJ = NC - 1
GROW = float(2.0 ** 100)
FULL = 255.0


class Plan:

    def __init__(self, nc, ctx, tag):
        self.nc, self.ctx, self.tag = nc, ctx, tag
        self.lines = {e: [] for e in ("sync", "scalar", "vector", "gpsimd", "tensor")}
        self.sems, self.count, self.at = {}, {}, {}

    def _sem(self, key):
        if key not in self.sems:
            self.sems[key] = self.ctx.enter_context(self.nc.semaphore(f"{self.tag}_{key}"))
            self.count[key] = 0
        return self.sems[key]

    def op(self, engine, fn, name=None, after=()):
        if name is not None:
            self._sem(engine)
            self.count[engine] += 1
            assert name not in self.at, name
            self.at[name] = (engine, self.count[engine])
        self.lines[engine].append((fn, tuple(after), (engine, 1) if name is not None else None))

    def dma(self, engine, slot, out, src, name, after=()):
        key = f"d_{slot}"
        self._sem(key)
        self.count[key] += 16
        assert name not in self.at, name
        self.at[name] = (key, self.count[key])
        self.lines[engine].append((lambda e: e.dma_start(out, src), tuple(after), (key, 16)))

    def end(self, engine, names):
        self.lines[engine].append((None, tuple(names), None))

    def emit(self, engine, eng):
        seen = {}
        for fn, after, sig in self.lines[engine]:
            for w in after:
                key, n = self.at[w]
                if seen.get(key, 0) < n:
                    seen[key] = n
                    eng.wait_ge(self.sems[key], n)
            if fn is None:
                continue
            inst = fn(eng)
            if sig is not None:
                inst.then_inc(self.sems[sig[0]], sig[1])


def run_block(nc, plan):
    with nc.Block() as block:
        @block.sync
        def _(e):
            plan.emit("sync", e)

        @block.scalar
        def _(e):
            plan.emit("scalar", e)

        @block.vector
        def _(e):
            plan.emit("vector", e)

        @block.gpsimd
        def _(e):
            plan.emit("gpsimd", e)

        @block.tensor
        def _(e):
            plan.emit("tensor", e)


def phase_weights(nc, io, g_hi, g_lo, r_hi, r_lo):
    with ExitStack() as ctx:
        def sb(name, shape, dt=F32):
            return ctx.enter_context(nc.sbuf_tensor(name, shape, dt))

        def pb(name, shape):
            return ctx.enter_context(nc.psum_tensor(name, shape, F32))

        wb = sb("wb", [128, NB, DX])
        nt = [sb(f"nt{i}", [128, D]) for i in range(2)]
        dl = [sb(f"dl{i}", [128, D]) for i in range(2)]
        wq = [sb(f"wq{i}", [128, D]) for i in range(2)]
        mk = [sb(f"mk{i}", [128, D], U8) for i in range(3)]
        lb = sb("lb", [128, 1024])
        la = [sb(f"la{i}", [128, 128]) for i in range(2)]
        ghs = [sb(f"ghs{i}", [128, 512], F32R) for i in range(2)]
        gls = [sb(f"gls{i}", [128, 512], F32R) for i in range(2)]
        sc = sb("sc", [128, NB * NB])
        rs = sb("rs", [128, NB * NB])
        idn = sb("idn", [128, 128])
        cb = sb("cb", [128, NC])
        cn = sb("cn", [128, NC])
        u = sb("u", [128, NC + 1])
        th = sb("th", [128, NJ])
        bj = sb("bj", [128, NJ])
        dj = sb("dj", [128, NJ])
        sm = sb("sm", [128, 2])
        acc = pb("acc", [128, D])
        pg = [pb(f"pg{i}", [128, 512]) for i in range(2)]
        pd = pb("pd", [128, 512])
        pr = pb("pr", [128, 512])

        pl = Plan(nc, ctx, "w")
        op, dma = pl.op, pl.dma

        s = ghs[0][:, 0:256].bitcast(F32)
        kf = ghs[0][:, 256:512].bitcast(F32)
        r = ghs[1][:, 0:256].bitcast(F32)
        p2 = ghs[1][:, 256:512].bitcast(F32)
        k1 = gls[0][:, 0:256].bitcast(I32)
        k2 = gls[0][:, 256:512].bitcast(I32)

        dma("sync", "cb", cb[:], io["cb"].partition_broadcast(128), "cb")
        dma("sync", "sl", sc[:], io["sl"], "sl")
        dma("sync", "lb", lb[:], io["lb"], "lb")
        for b in range(2):
            dma("sync", f"la{b}", la[b][:], io["la"][:, b * 128:(b + 1) * 128], f"la{b}")
            dma("sync", f"w{b}", nt[b][:], io["w"][b], f"w{b}")
        dma("sync", "id", idn[:], io["id"], "id")
        for t in range(NB):
            dma("sync", f"wb{t}", wb[:, t, :], io["wb"][t], f"wb{t}")

        step = [0]
        last = [None]

        def v(fn, after=()):
            n = f"v{step[0]}"
            step[0] += 1
            op("vector", fn, n, (*after, *([last[0]] if last[0] else [])))
            last[0] = n
            return n

        LOG2E, LN2H, LN2L = 1.4426950408889634, 0.693359375, -2.12194440054690581e-4
        v(lambda e: e.tensor_scalar(s, sc[:], 100.0, -110.0, ALU.min, ALU.max), ("sl",))
        v(lambda e: e.tensor_scalar(k2, s, LOG2E, None, ALU.mult))
        v(lambda e: e.tensor_copy(kf, k2))
        v(lambda e: e.scalar_tensor_tensor(r, kf, -LN2H, s, ALU.mult, ALU.add))
        v(lambda e: e.scalar_tensor_tensor(r, kf, -LN2L, r, ALU.mult, ALU.add))
        co = [1.0 / 40320, 1.0 / 5040, 1.0 / 720, 1.0 / 120, 1.0 / 24, 1.0 / 6, 0.5, 1.0, 1.0]
        v(lambda e: e.tensor_scalar(p2, r, co[0], co[1], ALU.mult, ALU.add))
        for c in co[2:]:
            v(lambda e: e.tensor_tensor(p2, p2, r, ALU.mult))
            v(lambda e, c=c: e.tensor_scalar(p2, p2, c, None, ALU.add))
        v(lambda e: e.tensor_scalar(k1, k2, 1, None, ALU.arith_shift_right))
        v(lambda e: e.tensor_tensor(k2, k2, k1, ALU.subtract))
        for k in (k1, k2):
            v(lambda e, k=k: e.tensor_scalar(k, k, 127.0, None, ALU.add))
            v(lambda e, k=k: e.tensor_scalar(k, k, 23, None, ALU.logical_shift_left))
        v(lambda e: e.tensor_tensor(p2, p2, gls[0][:, 0:256].bitcast(F32), ALU.mult))
        v(lambda e: e.tensor_tensor(sc[:], p2, gls[0][:, 256:512].bitcast(F32), ALU.mult))
        scale_ready = v(lambda e: e.reciprocal(rs[:], sc[:]))

        v(lambda e: e.tensor_scalar(cn[:], cb[:], -1.0, None, ALU.mult), ("cb",))
        v(lambda e: e.tensor_tensor(cn[:], cn[:], cb[:], ALU.max))
        v(lambda e: e.tensor_reduce(sm[:, 0:1], cn[:], AXX, ALU.max))
        v(lambda e: e.tensor_scalar(sm[:, 0:1], sm[:, 0:1], 1e-8, None, ALU.max))
        v(lambda e: e.reciprocal(sm[:, 1:2], sm[:, 0:1]))
        v(lambda e: e.tensor_scalar(cn[:], cb[:], sm[:, 1:2], None, ALU.mult))
        v(lambda e: e.tensor_tensor(th[:], cn[:, 0:NJ], cn[:, 1:NC], ALU.add))
        v(lambda e: e.tensor_scalar(th[:], th[:], 0.5, None, ALU.mult))
        v(lambda e: e.tensor_tensor(dj[:], cn[:, 1:NC], cn[:, 0:NJ], ALU.subtract))
        v(lambda e: e.tensor_scalar(dj[:], dj[:], 1.0 / FULL, None, ALU.mult))
        v(lambda e: e.memset(u[:, 0:1], -3e38))
        v(lambda e: e.memset(u[:, NC:NC + 1], 3e38))
        for g in (16, 8, 4, 2, 1):
            n = NC // (2 * g)
            e0, e1 = g, g + 2 * g * (n - 1) + 1
            v(lambda e, g=g, e0=e0, e1=e1: e.tensor_tensor(
                u[:, e0:e1:2 * g], th[:, e0 - 1:e1 - 1:2 * g], u[:, e0 - g:e1 - g:2 * g], ALU.max))
            v(lambda e, g=g, e0=e0, e1=e1: e.tensor_tensor(
                u[:, e0:e1:2 * g], u[:, e0:e1:2 * g], u[:, e0 + g:e1 + g:2 * g], ALU.min))
        book_ready = v(lambda e: e.tensor_scalar(bj[:], u[:, 1:NC], -GROW, None, ALU.mult))

        def grouped(t):
            return t.rearrange("p (a i) -> p a i", a=NB)

        def per_group(t, b):
            return t[:, b * NB:(b + 1) * NB].unsqueeze(2).to_broadcast([128, NB, 128])

        def delta_pe(b):
            for q in range(4):
                for k in range(4):
                    ot = 4 * q + k
                    h = 64 * (ot // 8)
                    after = []
                    if k == 0:
                        after += ["lb", f"la{b}"]
                        if q > 0:
                            after.append(f"dl{b}.{q - 1}")
                        elif b > 0:
                            after.append(f"dl{b - 1}.3")
                    op("tensor", lambda e, k=k, ot=ot, h=h: e.matmul(
                        pd[:, k * 128:(k + 1) * 128], lb[h:h + 64, (ot % 8) * 128:(ot % 8 + 1) * 128],
                        la[b % 2][h:h + 64, :], start=True, stop=True),
                        f"pd{b}.{q}" if k == 3 else None, after)

        def delta_act(b):
            for q in range(4):
                after = [f"pd{b}.{q}"]
                if b >= 2:
                    after.append(f"we{b - 2}")
                op("scalar", lambda e, q=q: e.activation(
                    dl[b % 2][:, q * 512:(q + 1) * 512], pd[:], ACT.Copy, scale=0.5), f"dl{b}.{q}", after)

        def normalise(b):
            op("gpsimd", lambda e: e.tensor_tensor(nt[b % 2][:], nt[b % 2][:], dl[b % 2][:], ALU.add),
               f"wg{b}", [f"w{b}", f"dl{b}.3"])
            op("gpsimd", lambda e: e.tensor_tensor(grouped(nt[b % 2][:]), grouped(nt[b % 2][:]),
                                                   per_group(rs, b), ALU.mult),
               f"n{b}", [f"wg{b}", scale_ready])

        def mask(b, j):
            k = NJ * b + j
            after = [f"n{b}", book_ready]
            if k >= 3:
                after.append(f"ac{(k - 3) // NJ}.{(k - 3) % NJ}")
            op("scalar", lambda e: e.activation(mk[k % 3][:], nt[b % 2][:], ACT.Identity,
                                                bias=bj[:, j:j + 1], scale=GROW), f"mk{b}.{j}", after)

        def add(b, j):
            k = NJ * b + j
            if j == 0:
                op("vector", lambda e: e.scalar_tensor_tensor(
                    acc[:], mk[k % 3][:], dj[:, 0:1], nt[b % 2][:], ALU.mult, ALU.subtract),
                    f"ac{b}.0", [f"mk{b}.0"] + ([f"q{b - 1}"] if b else []))
            else:
                op("vector", lambda e: e.scalar_tensor_tensor(
                    acc[:], mk[k % 3][:], dj[:, j:j + 1], acc[:], ALU.mult, ALU.add),
                    f"ac{b}.{j}", [f"mk{b}.{j}", f"ac{b}.{j - 1}"])

        def close(b):
            after = [f"ac{b}.{NJ - 1}"]
            if b >= 2:
                after.append(f"pr{b - 2}")
            op("vector", lambda e: e.scalar_tensor_tensor(
                wq[b % 2][:], acc[:], cn[:, 0:1], nt[b % 2][:], ALU.add, ALU.add), f"q{b}", after)

        def effective(b):
            op("gpsimd", lambda e: e.tensor_tensor(grouped(wq[b % 2][:]), grouped(wq[b % 2][:]),
                                                   per_group(sc, b), ALU.mult), f"ws{b}", [f"q{b}"])
            op("gpsimd", lambda e: e.tensor_tensor(wq[b % 2][:], wq[b % 2][:], dl[b % 2][:], ALU.add),
               f"we{b}", [f"ws{b}"])

        def product(b):
            for c in range(5):
                k = 4 * b + c
                if c < 4:
                    out, cols = pg[k % 2], slice(c * 512, (c + 1) * 512)
                    free = [f"gl{k - 2}"] if k >= 2 else []
                else:
                    out, cols = pr, slice(D, DX)
                    free = [f"rl{b - 1}"] if b else []
                own = c == b // 4
                for t in range(NB):
                    after = [f"wb{t}"]
                    if t == 0:
                        after += [f"we{b}", *free]
                    end = t == NB - 1 and not own
                    op("tensor", lambda e, t=t, out=out, cols=cols, end=end: e.matmul(
                        out[:, 0:cols.stop - cols.start], wq[b % 2][:, t * 128:(t + 1) * 128],
                        wb[:, t, cols], start=t == 0, stop=end),
                        (f"pg{k}" if c < 4 else f"pr{b}") if end else None, after)
                if own:
                    o = (b % 4) * 128
                    op("tensor", lambda e, out=out, o=o: e.matmul(
                        out[:, o:o + 128], idn[:], idn[:], start=False, stop=True), f"pg{k}", ["id"])

        def part_act(b, c):
            k = 4 * b + c
            op("scalar", lambda e: e.activation(ghs[k % 2][:], pg[k % 2][:], ACT.Copy), f"gh{k}",
               [f"pg{k}"] + ([f"sh{k - 2}", f"gl{k - 2}"] if k >= 2 else [scale_ready]))

        def part_dve(b, c):
            k = 4 * b + c
            op("vector", lambda e: e.tensor_tensor(gls[k % 2][:], pg[k % 2][:], ghs[k % 2][:].bitcast(F32),
                                                   ALU.subtract), f"gl{k}",
               [f"gh{k}"] + ([f"so{k - 2}"] if k >= 2 else []))

        def part_out(b, c):
            k = 4 * b + c
            dma("sync", f"sh{k % 2}", g_hi[b, :, c * 512:(c + 1) * 512], ghs[k % 2][:].bitcast(F32), f"sh{k}", [f"gh{k}"])
            dma("sync", f"so{k % 2}", g_lo[b, :, c * 512:(c + 1) * 512], gls[k % 2][:].bitcast(F32), f"so{k}", [f"gl{k}"])

        def route_act(b):
            op("scalar", lambda e: e.activation(r_hi[:, b, :], pr[:, 0:XW], ACT.Copy), f"rh{b}", [f"pr{b}"])

        def route_dve(b):
            op("vector", lambda e: e.tensor_tensor(r_lo[:, b, :], pr[:, 0:XW], r_hi[:, b, :].bitcast(F32),
                                                   ALU.subtract), f"rl{b}", [f"rh{b}"])

        delta_pe(0)
        delta_pe(1)
        for b in range(NB):
            if b + 2 < NB:
                delta_pe(b + 2)
            product(b)

        delta_act(0)
        delta_act(1)
        normalise(0)
        normalise(1)
        for b in range(NB):
            for j in range(NJ):
                if j == 2 and b >= 2:
                    part_act(b - 2, 3)
                    route_act(b - 2)
                if j == 6 and 2 <= b + 1 < NB:
                    delta_act(b + 1)
                if b >= 1 and j in (14, 20, 26):
                    part_act(b - 1, (j - 14) // 6)
                mask(b, j)
        for j in range(NJ * NB):
            b, jj = j // NJ, j % NJ
            if jj == 3 and b >= 2:
                part_dve(b - 2, 3)
                route_dve(b - 2)
            if b >= 1 and jj in (15, 21, 27):
                part_dve(b - 1, (jj - 15) // 6)
            add(b, jj)
            if jj == NJ - 1:
                close(b)
        part_act(NB - 2, 3)
        route_act(NB - 2)
        part_dve(NB - 2, 3)
        route_dve(NB - 2)
        for c in range(4):
            part_act(NB - 1, c)
            part_dve(NB - 1, c)
        route_act(NB - 1)
        route_dve(NB - 1)

        for b in range(NB):
            effective(b)
            if b + 2 < NB:
                normalise(b + 2)

        for b in range(NB + 1):
            if b >= 2:
                part_out(b - 2, 3)
            if b >= 1:
                for c in range(3):
                    part_out(b - 1, c)
            if b + 2 < NB:
                dma("sync", f"la{b % 2}", la[b % 2][:], io["la"][:, (b + 2) * 128:(b + 3) * 128], f"la{b + 2}",
                    [f"pd{b}.3"])
                dma("sync", f"w{b % 2}", nt[b % 2][:], io["w"][b + 2], f"w{b + 2}", [f"q{b}", f"mk{b}.{NJ - 1}"])
        part_out(NB - 1, 3)
        n = 4 * NB
        pl.end("sync", [f"sh{n - 2}", f"so{n - 2}", f"sh{n - 1}", f"so{n - 1}"])
        for e in ("vector", "tensor", "gpsimd", "scalar"):
            pl.end(e, [f"rl{NB - 1}"])
        run_block(nc, pl)


def phase_tokens(nc, io, g_hi, g_lo, b_half, r_hi, r_lo, out):
    with ExitStack() as ctx:
        def sb(name, shape, dt=F32):
            return ctx.enter_context(nc.sbuf_tensor(name, shape, dt))

        def pb(name, shape):
            return ctx.enter_context(nc.psum_tensor(name, shape, F32))

        H = D // 2
        gh = sb("gh", [128, NB, H], F32R)
        gl = sb("gl", [128, NB, H], F32R)
        xr = [sb(f"xr{i}", [128, D]) for i in range(2)]
        xh = [sb(f"xh{i}", [128, D], F32R) for i in range(2)]
        xl = [sb(f"xl{i}", [128, D], F32R) for i in range(2)]
        bs = sb("bs", [96, H], F32R)
        sa = [sb(f"sa{h}", [96, 128], F32R) for h in range(NT)]
        os_ = [sb(f"os{i}", [128, 512]) for i in range(2)]
        idn = sb("idn2", [128, 128])
        cr = sb("cr", [128, 96])
        ex = sb("ex", [128, NE])
        pe_ = sb("pe_", [128, NE])
        st = sb("st", [128, 4])
        z = sb("z", [128, 128])
        zt = sb("zt", [128, 128])
        po = [pb(f"po{i}", [128, 512]) for i in range(4)]
        ps = pb("ps", [128, 512])
        pz = pb("pz", [128, 512])
        pm = pb("pm", [128, 512])

        pl = Plan(nc, ctx, "t")
        op, dma = pl.op, pl.dma

        raw = xr[1]
        for k in (0, 32, 64):
            op("vector", lambda e, k=k: e.memset(cr[:, k:k + 32], 0.0), f"cr0.{k}")
            dma("sync", f"cr{k}", cr[:, k:k + NR], io["cores"], f"cr{k}", [f"cr0.{k}"])
        op("vector", lambda e: e.memset(raw[:], 0.0), "raw0")
        for k in (0, 32, 64):
            dma("sync", f"bw{k}", raw[k:k + NR, :], io["bw"], f"bw{k}", ["raw0"])
        for k in (0, 64):
            dma("sync", f"bb{k}", raw[k + NR:k + NR + 1, :], io["b"], f"bb{k}", ["raw0"])
        dma("sync", "id", idn[:], io["id"], "id")
        bw = xh[1]
        op("scalar", lambda e: e.activation(bw[0:96, :], raw[0:96, :], ACT.Copy), "bw.hi",
           ["bw0", "bw32", "bw64", "bb0", "bb64"])
        op("vector", lambda e: e.tensor_tensor(bw[64:96, :], raw[64:96, :], bw[64:96, :].bitcast(F32), ALU.subtract),
           "bw", ["bw.hi"])
        op("vector", lambda e: e.tensor_copy(bs[:], bw[0:96, 0:H].bitcast(F32)), "bs0", ["bw"])
        dma("sync", "bsd", b_half, bw[0:96, H:D].bitcast(F32), "bs.kept", ["bw"])
        for t in range(NT):
            op("gpsimd", lambda e, t=t: e.memset(sa[t][:].bitcast(F32), 1.0), f"s1.{t}", [f"s0.{t - 1}"] if t else [])
            op("gpsimd", lambda e, t=t: e.memset(sa[t][32:64, :].bitcast(F32), 0.0), f"s0.{t}", [f"s1.{t}"])

        tiles = [(h, t) for h in range(2) for t in range(NT)]

        def load_x(i):
            h, t = tiles[i]
            after = [f"xl{i - 2}"] if i >= 2 else []
            if i == 1:
                after = ["bw"]
            dma("sync", f"x{i % 2}", xr[i % 2][:], io["x"][t], f"x{i}", after)

        def load_g(h):
            for k in range(NB):
                after = [f"k{NT - 1}.{k}"] if h else []
                dma("sync", f"gh{k}", gh[:, k, :].bitcast(F32), g_hi[k, :, h * H:(h + 1) * H], f"gh{h}.{k}", after)
                dma("sync", f"gl{k}", gl[:, k, :].bitcast(F32), g_lo[k, :, h * H:(h + 1) * H], f"gl{h}.{k}", after)

        def split(i):
            op("scalar", lambda e: e.activation(xh[i % 2][:], xr[i % 2][:], ACT.Copy), f"xh{i}",
               [f"x{i}"] + ([f"pt{i - 2}"] if i >= 2 else ["bs0", "bs.kept"] if i == 1 else []))
            op("vector", lambda e: e.tensor_tensor(xl[i % 2][:], xr[i % 2][:], xh[i % 2][:].bitcast(F32), ALU.subtract),
               f"xl{i}", [f"xh{i}"] + ([f"pt{i - 2}"] if i >= 2 else []))

        def xs(x, k):
            return x[:, k * 128:(k + 1) * 128]

        def route_pe(i):
            a, b = xh[i % 2], xl[i % 2]
            n = 0
            for k in range(NB):
                for x, w in ((a, r_hi), (a, r_lo), (b, r_hi)):
                    n += 1
                    op("tensor", lambda e, x=x, w=w, k=k, n=n: e.matmul(
                        ps[:, 0:XW], xs(x, k), w[:, k, :], start=n == 1, stop=n == 3 * NB),
                        f"ps{i}" if n == 3 * NB else None,
                        [f"xl{i}"] + ([f"z{i - 1}"] if i else []) if n == 1 else [])

        def route_chain(i):
            lg = ps[:, NR:XW]
            op("vector", lambda e: e.tensor_reduce(st[:, 0:1], lg, AXX, ALU.max), f"mx{i}", [f"ps{i}"])
            op("vector", lambda e: e.tensor_scalar(st[:, 1:2], st[:, 0:1], -1.0, None, ALU.mult), f"nm{i}", [f"mx{i}"])
            op("scalar", lambda e: e.activation(ex[:], lg, ACT.Exp, bias=st[:, 1:2], scale=1.0), f"ex{i}", [f"nm{i}"])
            op("vector", lambda e: e.tensor_reduce(st[:, 2:3], ex[:], AXX, ALU.add), f"sm{i}", [f"ex{i}"])
            op("vector", lambda e: e.reciprocal(st[:, 3:4], st[:, 2:3]), f"rc{i}", [f"sm{i}"])
            op("vector", lambda e: e.tensor_scalar(pe_[:], ex[:], st[:, 3:4], 2.0, ALU.mult, ALU.mult), f"pr{i}", [f"rc{i}"])
            op("vector", lambda e: e.tensor_tensor(
                z[:].rearrange("p (a r) -> p a r", a=NE), pe_[:].unsqueeze(2).to_broadcast([128, NE, NR]),
                ps[:, 0:NR].unsqueeze(1).to_broadcast([128, NE, NR]), ALU.mult), f"z{i}",
                [f"pr{i}"] + ([f"pz{i - 1}"] if i else []))

        def turn_pe(i):
            op("tensor", lambda e: e.transpose(pz[:, 0:128], z[:], idn[:]), f"pz{i}",
               [f"z{i}", "id"] + ([f"zt{i - 1}"] if i else []))

        def turn_act(i):
            op("scalar", lambda e: e.activation(zt[:], pz[:, 0:128], ACT.Copy), f"zt{i}",
               [f"pz{i}"] + ([f"pm{i - 1}"] if i else []))

        def mix_pe(i):
            op("tensor", lambda e: e.matmul(pm[0:96, 0:128], cr[:], zt[:], start=True, stop=True), f"pm{i}",
               [f"zt{i}", "cr0", "cr32", "cr64"] + ([f"ml{i - 1}"] if i else []))

        def mix_out(i):
            for k in (0, 32, 64):
                op("scalar", lambda e, k=k: e.activation(sa[i][k:k + NR, :], pm[k:k + NR, 0:128], ACT.Copy),
                   f"mh{i}.{k}", [f"pm{i}", f"s0.{i}"])
            op("vector", lambda e: e.tensor_tensor(sa[i][32:32 + NR, :], pm[32:32 + NR, 0:128],
                                                   sa[i][32:32 + NR, :].bitcast(F32), ALU.subtract),
               f"ml{i}", [f"mh{i}.64"])

        def main_pe(i, k0, k1):
            h = i // NT
            for k in range(k0, k1):
                a, b = xh[i % 2], xl[i % 2]
                n = 0
                for x, w in ((a, gh), (a, gl), (b, gh)):
                    for c in range(2):
                        n += 1
                        after = [f"xl{i}", f"gh{h}.{k}", f"gl{h}.{k}"] if n == 1 else []
                        if k == 0 and n <= 2 and i >= 2:
                            after.append(f"o{i - 2}.{c}")
                        op("tensor", lambda e, x=x, w=w, c=c, k=k, n=n: e.matmul(
                            po[2 * (i % 2) + c][:], xs(x, k), w[:, k, c * 512:(c + 1) * 512],
                            start=k == 0 and n <= 2, stop=False),
                            f"k{i}.{k}" if n == 6 and i == NT - 1 else None, after)

        def low_pe(i):
            h, t = tiles[i]
            for c in range(2):
                op("tensor", lambda e, c=c: e.matmul(
                    po[2 * (i % 2) + c][:], sa[t][:], bs[:, c * 512:(c + 1) * 512],
                    start=False, stop=True), f"pt{i}" if c else f"pt{i}.0", [f"ml{t}", f"bs{h}"])

        def evacuate(i):
            free = lambda c: [f"st{i - 1}.{c}"] if i else []
            op("scalar", lambda e: e.activation(os_[0][:], po[2 * (i % 2)][:], ACT.Copy), f"o{i}.0",
               [f"pt{i}"] + free(0))
            op("vector", lambda e: e.tensor_copy(os_[1][:], po[2 * (i % 2) + 1][:]), f"o{i}.1", [f"pt{i}"] + free(1))

        def store(i):
            h, t = tiles[i]
            for c in range(2):
                dma("sync", f"st{c}", out[t, :, h * H + c * 512:h * H + (c + 1) * 512], os_[c][:], f"st{i}.{c}",
                    [f"o{i}.{c}"])

        N = len(tiles)
        load_x(0)
        load_g(0)
        load_x(1)
        split(0)
        for i in range(N):
            first = i < NT
            if first:
                route_pe(i)
                main_pe(i, 0, 6)
                turn_pe(i)
                main_pe(i, 6, 11)
                mix_pe(i)
                main_pe(i, 11, NB)
            else:
                main_pe(i, 0, NB)
            low_pe(i)
            if first:
                route_chain(i)
                turn_act(i)
                mix_out(i)
            if i:
                evacuate(i - 1)
            if i + 1 < N:
                split(i + 1)
            if i == NT - 1:
                load_g(1)
                dma("sync", "bsd", bs[:].bitcast(F32), b_half, "bs1", [f"pt{i}", "bs.kept"])
            if i + 2 < N:
                load_x(i + 2)
            if i:
                store(i - 1)
        evacuate(N - 1)
        store(N - 1)
        pl.end("sync", [f"st{N - 1}.0", f"st{N - 1}.1"])
        run_block(nc, pl)


def build(nc, io, out):
    g_hi = nc.dram_tensor("g_hi", [NB, 128, D], F32, kind="Internal").ap()
    g_lo = nc.dram_tensor("g_lo", [NB, 128, D], F32, kind="Internal").ap()
    b_half = nc.dram_tensor("b_half", [96, D // 2], F32, kind="Internal").ap()
    with ExitStack() as ctx:
        r_hi = ctx.enter_context(nc.sbuf_tensor("r_hi", [128, NB, XW], F32R))
        r_lo = ctx.enter_context(nc.sbuf_tensor("r_lo", [128, NB, XW], F32R))
        phase_weights(nc, io, g_hi, g_lo, r_hi, r_lo)
        phase_tokens(nc, io, g_hi, g_lo, b_half, r_hi, r_lo, out)


def kernel(x, condB_codebook, L0_cond_weight, L0_cond_scale_log, L0_cond_lora_A, L0_cond_lora_B, L0_ffn_W_base,
           L0_ffn_b_base, L0_ffn_A_w, L0_ffn_B_w, L0_ffn_router_w, L0_ffn_cores):
    import concourse.bacc as bacc
    from concourse.bass_utils import run_bass_kernel_spmd

    def lay(a):
        return np.ascontiguousarray(a)

    x = np.asarray(x)
    wide = np.concatenate([np.asarray(L0_ffn_W_base), np.asarray(L0_ffn_A_w), np.asarray(L0_ffn_router_w)], axis=0)
    la = np.asarray(L0_cond_lora_A)
    arrays = {
        "x": lay(x.reshape(NT, 128, NB, 128).transpose(0, 3, 2, 1).reshape(NT, 128, D)),
        "w": lay(np.asarray(L0_cond_weight).reshape(NB, 128, NB, 128).transpose(2, 1, 0, 3).reshape(NB, 128, D)),
        "sl": lay(np.asarray(L0_cond_scale_log).reshape(NB, 128, NB).transpose(1, 2, 0).reshape(128, NB * NB)),
        "lb": lay(np.asarray(L0_cond_lora_B).reshape(2, 1024, 64).transpose(0, 2, 1).reshape(128, 1024)),
        "la": lay(np.concatenate([la, la], axis=0)),
        "wb": lay(wide.T.reshape(NB, 128, DX)),
        "cores": lay(np.asarray(L0_ffn_cores).reshape(128, NR)),
        "bw": lay(np.asarray(L0_ffn_B_w).T),
        "b": lay(np.asarray(L0_ffn_b_base).reshape(1, D)),
        "cb": lay(np.asarray(condB_codebook)),
        "id": np.eye(128, dtype=np.float32),
    }
    nc = bacc.Bacc("TRN2", target_bir_lowering=False, num_devices=1)
    io = {k: nc.dram_tensor(f"in_{k}", a.shape, F32, kind="ExternalInput").ap() for k, a in arrays.items()}
    out = nc.dram_tensor("out", [NT, 128, D], F32, kind="ExternalOutput").ap()
    build(nc, io, out)
    r = run_bass_kernel_spmd(nc, [{f"in_{k}": a for k, a in arrays.items()}], core_ids=[0])
    return r.results[0]["out"].reshape(32, 128, D)
```

```python
import numpy as np
from contextlib import ExitStack

import concourse.bass as bass
import concourse.mybir as mybir

F32 = mybir.dt.float32
F32R = mybir.dt.float32r
I32 = mybir.dt.int32
U8 = mybir.dt.uint8
ALU = mybir.AluOpType
ACT = mybir.ActivationFunctionType
AXX = mybir.AxisListType.X

D = 2048
NB = 16
NT = 32
NE = 8
NR = 16
XW = NE + NR
DX = D + XW
NC = 32
NJ = NC - 1
NP = 6
NM = 3
NW = 3
SPARE_AT = (0, 3, 9, 13, 17, 21)
DELTA_AT = (5, 6, 8, 9)
PART_AT = (12, 16, 19, 24)
CUT = (0, 384, 768, 1152, 1664, DX)
NV = NJ - NP
XM = 66
GROW = float(2.0 ** 100)
FULL = 255.0


class Plan:

    def __init__(self, nc, ctx):
        self.nc, self.ctx = nc, ctx
        self.lines = {e: [] for e in ("sync", "scalar", "vector", "gpsimd", "tensor")}
        self.sems, self.count, self.at = {}, {}, {}

    def _sem(self, key):
        if key not in self.sems:
            self.sems[key] = self.ctx.enter_context(self.nc.semaphore(f"s_{key}"))
            self.count[key] = 0
        return self.sems[key]

    def op(self, engine, fn, name=None, after=()):
        if name is not None:
            self._sem(engine)
            self.count[engine] += 1
            assert name not in self.at, name
            self.at[name] = (engine, self.count[engine])
        self.lines[engine].append((fn, tuple(after), (engine, 1) if name is not None else None))

    def dma(self, engine, slot, out, src, name, after=()):
        key = f"d_{slot}"
        self._sem(key)
        self.count[key] += 16
        assert name not in self.at, name
        self.at[name] = (key, self.count[key])
        self.lines[engine].append((lambda e: e.dma_start(out, src), tuple(after), (key, 16)))

    def end(self, engine, names):
        self.lines[engine].append((None, tuple(names), None))

    def emit(self, engine, eng):
        seen = {}
        for fn, after, sig in self.lines[engine]:
            for w in after:
                key, n = self.at[w]
                if seen.get(key, 0) < n:
                    seen[key] = n
                    eng.wait_ge(self.sems[key], n)
            if fn is None:
                continue
            inst = fn(eng)
            if sig is not None:
                inst.then_inc(self.sems[sig[0]], sig[1])


def run_block(nc, plan):
    with nc.Block() as block:
        @block.sync
        def _(e):
            plan.emit("sync", e)

        @block.scalar
        def _(e):
            plan.emit("scalar", e)

        @block.vector
        def _(e):
            plan.emit("vector", e)

        @block.gpsimd
        def _(e):
            plan.emit("gpsimd", e)

        @block.tensor
        def _(e):
            plan.emit("tensor", e)


class Room:

    def __init__(self, nc, ctx):
        self.nc = nc
        self.top = self.low = -(-nc.sbuf_base // 32) * 32
        H = D // 2
        at_wb = self.top
        self.wb = [self.take(f"wb{k}", DX) for k in range(NB)]
        at_nt = self.top
        self.nt = [self.take(f"nt{k}", D) for k in range(NW)]
        at_dl = self.top
        self.dl = [self.take(f"dl{k}", D) for k in range(2)]
        at_pp = self.top
        self.pp = self.take("pp", D)
        self.mk = [self.take(f"mk{k}", D, U8) for k in range(NM)]
        self.mp = [self.take(f"mp{k}", D, U8) for k in range(2)]
        self.tm = self.take("tm", H)
        at_gs = self.top
        self.gs = [self.take(f"gs{k}", 512) for k in range(2)]
        self.lb = self.take("lb", H)
        at_la = self.top
        self.la = [self.take(f"la{k}", 128) for k in range(2)]
        at_sc = self.top
        self.sc = self.take("sc", NB * NB)
        self.rs = self.take("rs", NB * NB)
        self.idn = self.take("idn", 128)
        self.cb = self.take("cb", NC)
        self.cn = self.take("cn", NC)
        self.u = self.take("u", NC + 1)
        self.th = self.take("th", NJ)
        self.bj = self.take("bj", NJ)
        self.dj = self.take("dj", NJ)
        self.sm = self.take("sm", 2)
        self.r_raw = self.take("r_raw", NB * XW).rearrange("p (k r) -> p k r", k=NB)

        self.gh, self.gw, self.gl = [], [], []
        for k in range(NB):
            at = at_wb + k * DX * 4
            self.gh.append(self.put(f"gh{k}", at, H, F32R))
            self.gw.append(self.put(f"gw{k}", at + H * 4, H))
            self.gl.append(self.put(f"gl{k}", at + H * 4, H, F32R))
        self.os = [self.put(f"os{k}", at_nt + k * 2048, 512) for k in range(4)]
        self.last = self.put("last", at_nt + H * 4, H)
        at_x = [(at_dl + D * 4, at_dl), (at_nt + D * 4, at_nt + 2 * D * 4)]
        self.xh = [self.put(f"xh{k}", a, D, F32R) for k, (a, _) in enumerate(at_x)]
        self.xw = [self.put(f"xw{k}", a, D) for k, (_, a) in enumerate(at_x)]
        self.xl = [self.put(f"xl{k}", a, D, F32R) for k, (_, a) in enumerate(at_x)]
        self.bw = self.put("bw", at_nt + D * 4, D)
        self.sa = [self.put(f"sa{k}", at_pp + k * 512, 128, F32R, 96) for k in range(NT)]
        self.rr = self.put("rr", at_pp + NT * 512, NB * XM, F32R).rearrange("p (k r) -> p k r", k=NB)
        assert at_pp + NT * 512 + NB * XM * 4 <= at_gs
        self.bs = self.put("bs", at_gs, D, F32R, 96)
        self.pj = self.put("pj", at_la, 128, F32, 2 * XW)
        self.z = self.put("z", at_la + 512, 128)
        self.cr = self.put("cr", at_sc, 96)
        self.se = self.put("se", at_sc + 384, XW, F32, 2 * XW)
        self.ex = self.put("ex", at_sc + 512, NE)
        self.pe = self.put("pe", at_sc + 544, NE)
        self.st = self.put("st", at_sc + 576, 4)

        def bank(name, n):
            return ctx.enter_context(nc.psum_tensor(name, [128, n * 512], F32))[:]

        self.acc = bank("acc", 4)
        self.pg = [bank(f"pg{k}", 1) for k in range(2)]
        self.pd = [bank(f"pd{k}", 1) for k in range(2)]
        self.po = [self.acc[:, k * 512:(k + 1) * 512] for k in range(4)]

    def put(self, name, at, n, dtype=F32, rows=128):
        return self.nc.alloc_sbuf_tensor_at(name, [rows, n], dtype, offset=at)[:]

    def take(self, name, n, dtype=F32):
        at = self.top
        self.top += -(-n * (1 if dtype is U8 else 4) // 32) * 32
        return self.put(name, at, n, dtype)


def plan_weights(pl, room, io, g_raw):
    op, dma = pl.op, pl.dma
    wb, nt, dl, pp, mk, mp, tm, gs, lb, la = (room.wb, room.nt, room.dl, room.pp, room.mk, room.mp, room.tm, room.gs,
                                              room.lb, room.la)
    sc, rs, idn, cb, cn, u, th, bj, dj, sm = (room.sc, room.rs, room.idn, room.cb, room.cn, room.u, room.th, room.bj,
                                              room.dj, room.sm)
    r_raw, acc, pg, pd = room.r_raw, room.acc, room.pg, room.pd

    s = pp[:, 0:256]
    kf = pp[:, 256:512]
    r = pp[:, 512:768]
    p2 = pp[:, 768:1024]
    k1 = pp[:, 1024:1280].bitcast(I32)
    k2 = pp[:, 1280:1536].bitcast(I32)

    dma("sync", "sl", sc, io["sl"], "sl")
    dma("sync", "lb", lb, io["lb"], "lb")
    dma("sync", "la0", la[0], io["la"][:, 0:128], "la0")
    dma("sync", "cb", cb, io["cb"].partition_broadcast(128), "cb")
    dma("sync", "w0", nt[0], io["w"][0], "w0")
    dma("sync", "la1", la[1], io["la"][:, 128:256], "la1")
    for b in range(1, NW):
        dma("sync", f"w{b}", nt[b], io["w"][b], f"w{b}")
    dma("sync", "id", idn, io["id"], "id")
    for t in range(NB):
        dma("sync", f"wb{t}", wb[t], io["wb"][t], f"wb{t}")

    chains = {"es": [], "bk": []}

    def step(chain, fn, after=()):
        steps = chains[chain]
        steps.append((fn, after))
        return f"{chain}{len(steps) - 1}"

    def v(fn, after=()):
        return step("es", fn, after)

    def w(fn, after=()):
        return step("bk", fn, after)

    LOG2E, LN2H, LN2L = 1.4426950408889634, 0.693359375, -2.12194440054690581e-4
    v(lambda e: e.tensor_scalar(s, sc, 100.0, -110.0, ALU.min, ALU.max), ("sl",))
    v(lambda e: e.tensor_scalar(k2, s, LOG2E, None, ALU.mult))
    v(lambda e: e.tensor_copy(kf, k2))
    v(lambda e: e.scalar_tensor_tensor(r, kf, -LN2H, s, ALU.mult, ALU.add))
    v(lambda e: e.scalar_tensor_tensor(r, kf, -LN2L, r, ALU.mult, ALU.add))
    co = [1.0 / 40320, 1.0 / 5040, 1.0 / 720, 1.0 / 120, 1.0 / 24, 1.0 / 6, 0.5, 1.0, 1.0]
    v(lambda e: e.tensor_scalar(p2, r, co[0], co[1], ALU.mult, ALU.add))
    for c in co[2:]:
        v(lambda e: e.tensor_tensor(p2, p2, r, ALU.mult))
        v(lambda e, c=c: e.tensor_scalar(p2, p2, c, None, ALU.add))
    v(lambda e: e.tensor_scalar(k1, k2, 1, None, ALU.arith_shift_right))
    v(lambda e: e.tensor_tensor(k2, k2, k1, ALU.subtract))
    for k in (k1, k2):
        v(lambda e, k=k: e.tensor_scalar(k, k, 127.0, None, ALU.add))
        v(lambda e, k=k: e.tensor_scalar(k, k, 23, None, ALU.logical_shift_left))
    v(lambda e: e.tensor_tensor(p2, p2, pp[:, 1024:1280], ALU.mult))
    v(lambda e: e.tensor_tensor(sc, p2, pp[:, 1280:1536], ALU.mult))
    scale_first = v(lambda e: e.reciprocal(rs[:, 0:NB], sc[:, 0:NB]))
    scale_ready = v(lambda e: e.reciprocal(rs[:, NB:], sc[:, NB:]))

    w(lambda e: e.tensor_scalar(cn, cb, -1.0, None, ALU.mult), ("cb",))
    w(lambda e: e.tensor_tensor(cn, cn, cb, ALU.max))
    w(lambda e: e.tensor_reduce(sm[:, 0:1], cn, AXX, ALU.max))
    w(lambda e: e.tensor_scalar(sm[:, 0:1], sm[:, 0:1], 1e-8, None, ALU.max))
    w(lambda e: e.reciprocal(sm[:, 1:2], sm[:, 0:1]))
    w(lambda e: e.tensor_scalar(cn, cb, sm[:, 1:2], None, ALU.mult))
    w(lambda e: e.tensor_tensor(th, cn[:, 0:NJ], cn[:, 1:NC], ALU.add))
    w(lambda e: e.tensor_scalar(th, th, 0.5, None, ALU.mult))
    w(lambda e: e.tensor_tensor(dj, cn[:, 1:NC], cn[:, 0:NJ], ALU.subtract))
    w(lambda e: e.tensor_scalar(dj, dj, 1.0 / FULL, None, ALU.mult))
    w(lambda e: e.memset(u[:, 0:1], -3e38))
    w(lambda e: e.memset(u[:, NC:NC + 1], 3e38))
    for g in (16, 8, 4, 2, 1):
        n = NC // (2 * g)
        e0, e1 = g, g + 2 * g * (n - 1) + 1
        w(lambda e, g=g, e0=e0, e1=e1: e.tensor_tensor(
            u[:, e0:e1:2 * g], th[:, e0 - 1:e1 - 1:2 * g], u[:, e0 - g:e1 - g:2 * g], ALU.max))
        w(lambda e, g=g, e0=e0, e1=e1: e.tensor_tensor(
            u[:, e0:e1:2 * g], u[:, e0:e1:2 * g], u[:, e0 + g:e1 + g:2 * g], ALU.min))
    book_ready = w(lambda e: e.tensor_scalar(bj, u[:, 1:NC], -GROW, None, ALU.mult))
    for k in range(max(len(steps) for steps in chains.values())):
        for chain, steps in chains.items():
            if k < len(steps):
                fn, after = steps[k]
                op("vector", fn, f"{chain}{k}", (*after, *([f"{chain}{k - 1}"] if k else [])))

    def grouped(t):
        return t.rearrange("p (a i) -> p a i", a=NB)

    def per_group(t, b):
        return t[:, b * NB:(b + 1) * NB].unsqueeze(2).to_broadcast([128, NB, 128])

    def delta_pe(b, q):
        n = 4 * b + q
        for k in range(4):
            ot = 4 * q + k
            h = 64 * (ot // 8)
            after = []
            if k == 0:
                after = ["lb", f"la{b}"] + ([f"dl{(n - 2) // 4}.{(n - 2) % 4}"] if n >= 2 else [])
            op("tensor", lambda e, k=k, ot=ot, h=h: e.matmul(
                pd[n % 2][:, k * 128:(k + 1) * 128], lb[h:h + 64, (ot % 8) * 128:(ot % 8 + 1) * 128],
                la[b % 2][h:h + 64, :], start=True, stop=True),
                f"pd{b}.{q}" if k == 3 else None, after)

    def delta_act(b, q):
        op("scalar", lambda e: e.activation(
            dl[b % 2][:, q * 512:(q + 1) * 512], pd[(4 * b + q) % 2], ACT.Copy, scale=0.5), f"dl{b}.{q}",
           [f"pd{b}.{q}"] + ([f"we{b - 2}"] if b >= 2 else []))

    def normalise(b):
        for q in range(4 if b == 0 else 1):
            cols = slice(q * 512, (q + 1) * 512) if b == 0 else slice(0, D)
            op("gpsimd", lambda e, cols=cols: e.tensor_tensor(
                nt[b % NW][:, cols], nt[b % NW][:, cols], dl[b % 2][:, cols], ALU.add),
               f"wg{b}" if q == 3 or b else f"wg{b}.{q}", [f"w{b}", f"dl{b}.{3 if b else q}"])
        op("gpsimd", lambda e: e.tensor_tensor(grouped(nt[b % NW]), grouped(nt[b % NW]),
                                               per_group(rs, b), ALU.mult),
           f"n{b}", [f"wg{b}", scale_ready if b else scale_first])

    HD = D // 2

    def spare_mask(b, i):
        k = NP * b + i
        after = [f"n{b}", book_ready]
        if k >= 2:
            after.append(f"pp{(k - 2) // NP}.{(k - 2) % NP}.1")
        op("scalar", lambda e: e.activation(mp[k % 2], nt[b % NW], ACT.Identity,
                                            bias=bj[:, NV + i:NV + i + 1], scale=GROW), f"mp{b}.{i}", after)

    def spare(b, i):
        k, j = NP * b + i, NV + i
        for h in range(2):
            cols = slice(h * HD, (h + 1) * HD)
            after = [f"mp{b}.{i}", book_ready]
            if k or h:
                kk = 2 * k + h - 1
                after.append(f"pp{kk // 2 // NP}.{kk // 2 % NP}.{kk % 2}")
            op("gpsimd", lambda e, cols=cols: e.tensor_scalar(
                tm, mp[k % 2][:, cols], dj[:, j:j + 1], 0.0, ALU.mult, ALU.add), f"tm{b}.{i}.{h}", after)
            src = pp if i else nt[b % NW]
            op("gpsimd", lambda e, cols=cols: e.tensor_tensor(pp[:, cols], src[:, cols], tm, ALU.add),
               f"pp{b}.{i}.{h}", [f"tm{b}.{i}.{h}"] + ([f"q{b - 1}"] if b and i == 0 else []))

    def mask(b, j):
        k = NV * b + j
        after = [f"n{b}", book_ready]
        if k >= NM:
            after.append(f"ac{(k - NM) // NV}.{(k - NM) % NV}.1")
        op("scalar", lambda e: e.activation(mk[k % NM], nt[b % NW], ACT.Identity,
                                            bias=bj[:, j:j + 1], scale=GROW), f"mk{b}.{j}", after)

    def add(b, j):
        k = NV * b + j
        for h in range(2):
            cols = slice(h * HD, (h + 1) * HD)
            if j == 0:
                op("vector", lambda e, cols=cols: e.scalar_tensor_tensor(
                    acc[:, cols], mk[k % NM][:, cols], dj[:, 0:1], nt[b % NW][:, cols], ALU.mult, ALU.subtract),
                    f"ac{b}.0.{h}", [f"mk{b}.0"] + ([f"q{b - 1}"] if b else []))
            else:
                op("vector", lambda e, cols=cols: e.scalar_tensor_tensor(
                    acc[:, cols], mk[k % NM][:, cols], dj[:, j:j + 1], acc[:, cols], ALU.mult, ALU.add),
                    f"ac{b}.{j}.{h}", [f"mk{b}.{j}", f"ac{b}.{j - 1}.{h}"])

    def close(b):
        op("vector", lambda e: e.scalar_tensor_tensor(
            nt[b % NW], acc, cn[:, 0:1], pp, ALU.add, ALU.add), f"q{b}",
           [f"ac{b}.{NV - 1}.1", f"mk{b}.{NV - 1}", f"pp{b}.{NP - 1}.1"])

    def effective(b):
        op("gpsimd", lambda e: e.tensor_tensor(grouped(nt[b % NW]), grouped(nt[b % NW]), per_group(sc, b), ALU.mult),
           f"ws{b}", [f"q{b}"])
        op("gpsimd", lambda e: e.tensor_tensor(nt[b % NW], nt[b % NW], dl[b % 2], ALU.add), f"we{b}", [f"ws{b}"])

    def effective_last(b):
        for q in range(4):
            cols = slice(q * 512, (q + 1) * 512)
            op("gpsimd", lambda e, q=q, cols=cols: e.tensor_tensor(
                nt[b % NW][:, cols].rearrange("p (a i) -> p a i", a=4), nt[b % NW][:, cols].rearrange("p (a i) -> p a i", a=4),
                sc[:, b * NB + 4 * q:b * NB + 4 * q + 4].unsqueeze(2).to_broadcast([128, 4, 128]), ALU.mult),
                f"ws{b}.{q}", [f"q{b}"])
            op("gpsimd", lambda e, cols=cols: e.tensor_tensor(
                nt[b % NW][:, cols], nt[b % NW][:, cols], dl[b % 2][:, cols], ALU.add), f"we{b}.{q}", [f"ws{b}.{q}"])

    def product(b):
        for c in range(5):
            k = 5 * b + c
            c0, c1 = CUT[c], CUT[c + 1]
            out = pg[k % 2]
            own = c0 <= b * 128 < c1
            for t in range(NB):
                if b + 2 < NB and c == 0 and t in (5, 10):
                    delta_pe(b + 2, 2 + (t == 10))
                after = [f"wb{t}"]
                if t == 0:
                    after += [f"we{b}"] + ([f"ge{k - 2}"] if k >= 2 else [])
                end = t == NB - 1 and not own
                op("tensor", lambda e, t=t, out=out, c0=c0, c1=c1, end=end: e.matmul(
                    out[:, 0:c1 - c0], nt[b % NW][:, t * 128:(t + 1) * 128],
                    wb[t][:, c0:c1], start=t == 0, stop=end), f"pg{k}" if end else None, after)
            if own:
                o = b * 128 - c0
                op("tensor", lambda e, out=out, o=o: e.matmul(
                    out[:, o:o + 128], idn, idn, start=False, stop=True), f"pg{k}", ["id"])

    def product_last(b):
        for t in range(NB):
            for c in range(5):
                k = 5 * b + c
                c0, c1 = CUT[c], CUT[c + 1]
                out = room.po[c] if c < 4 else pg[k % 2]
                after = [f"we{b}.{t // 4}"] if t % 4 == 0 and c == 0 else []
                if c == 4 and t == 0:
                    after.append(f"ge{k - 6}")
                op("tensor", lambda e, t=t, out=out, c0=c0, c1=c1, c=c: e.matmul(
                    out[:, 0:c1 - c0], nt[b % NW][:, t * 128:(t + 1) * 128], wb[t][:, c0:c1],
                    start=t == 0, stop=t == NB - 1 and c < 4),
                    f"pg{k}" if t == NB - 1 and c < 4 else f"slice{t}" if c == 4 else None, after)
        o = b * 128 - CUT[4]
        op("tensor", lambda e: e.matmul(pg[k % 2][:, o:o + 128], idn, idn, start=False, stop=True), f"pg{k}")

    def part_act(b, c):
        k = 5 * b + c
        n = min(CUT[c + 1], D) - CUT[c]
        if c == 4:
            op("scalar", lambda e: e.activation(r_raw[:, b, :], pg[k % 2][:, n:n + XW], ACT.Copy), f"re{b}",
               [f"pg{k}"])
        op("scalar", lambda e: e.activation(gs[k % 2][:, 0:n], pg[k % 2][:, 0:n], ACT.Copy), f"ge{k}",
           [f"pg{k}"] + ([f"sg{k - 2}"] if k >= 2 else []))

    def part_out(b, c):
        k = 5 * b + c
        c0, c1 = CUT[c], min(CUT[c + 1], D)
        dma("sync", f"sg{k % 2}", g_raw[b, :, c0:c1], gs[k % 2][:, 0:c1 - c0], f"sg{k}", [f"ge{k}"])

    for b in range(2):
        for q in range(4):
            delta_pe(b, q)
    for b in range(NB):
        if b + 2 < NB:
            delta_pe(b + 2, 0)
            delta_pe(b + 2, 1)
        if b + 1 < NB:
            product(b)
    product_last(NB - 1)

    for b in range(2):
        for q in range(4):
            delta_act(b, q)
    normalise(0)
    normalise(1)
    for b in range(NB):
        for j in range(NV):
            if j == 4 and b >= 2:
                part_act(b - 2, 4)
            if j in DELTA_AT and 2 <= b + 1 < NB:
                delta_act(b + 1, DELTA_AT.index(j))
            if b >= 1 and j in PART_AT:
                part_act(b - 1, PART_AT.index(j))
            mask(b, j)
            if j in SPARE_AT:
                spare_mask(b, SPARE_AT.index(j))
            add(b, j)
        close(b)
    part_act(NB - 2, 4)

    for b in range(NB):
        if b:
            effective(b - 1)
        for i in range(NP):
            if i == 2 and 1 <= b < NB - 1:
                normalise(b + 1)
            spare(b, i)
    effective_last(NB - 1)

    for b in range(NB):
        if b >= 2:
            part_out(b - 2, 4)
        if b >= 1:
            for c in range(4):
                part_out(b - 1, c)
        if b + 2 < NB:
            dma("sync", f"la{b % 2}", la[b % 2], io["la"][:, (b + 2) * 128:(b + 3) * 128], f"la{b + 2}",
                [f"pd{b}.3"])
        if b >= 1 and b + 2 < NB:
            dma("sync", f"w{(b - 1) % NW}", nt[(b - 1) % NW], io["w"][b + 2], f"w{b + 2}", [f"pg{5 * b - 1}"])
    part_out(NB - 2, 4)


def plan_tokens(pl, room, io, g_raw, out):
    op, dma = pl.op, pl.dma
    H = D // 2
    gh, gl, gw, xh, xl, xw, bs, sa, os_ = (room.gh, room.gl, room.gw, room.xh, room.xl, room.xw, room.bs, room.sa,
                                           room.os)
    idn, cr, rr, pj, se, ex, pe_, st, z, zt = (room.idn, room.cr, room.rr, room.pj, room.se, room.ex, room.pe,
                                               room.st, room.z, room.z)
    r_raw, raw, acc = room.r_raw, room.bw, room.acc
    po, pp, ps, pz, pm = room.po, room.pd[0], room.pd[1], room.pg[0], room.pg[1]
    B = NB - 1
    last_we = f"we{B}.3"
    tiles = [(0, t) for t in range(NT)] + [(1, t) for t in (NT - 2, NT - 1, *range(NT - 2))]
    N = len(tiles)

    def kept(i):
        return i - 2 if i in (NT, NT + 1) else i

    def load_x(i):
        free = [f"pt{i - 2}"] if i >= 2 else ["we14"] if i == 0 else ["pg74"]
        for h in range(2):
            cols = slice(h * H, (h + 1) * H)
            dma("sync", f"x{i % 2}.{h}", xw[i % 2][:, cols], io["x"][tiles[i][1], :, cols], f"x{i}.{h}", free)

    def split(i):
        free = [f"pt{i - 2}"] if i >= 2 else [last_we] if i == 0 else ["bs"]
        for h in range(2):
            cols = slice(h * H, (h + 1) * H)
            op("scalar", lambda e, cols=cols: e.activation(xh[i % 2][:, cols], xw[i % 2][:, cols], ACT.Copy),
               f"xh{i}.{h}", [f"x{i}.{h}", *free])
            op("vector", lambda e, cols=cols: e.tensor_tensor(
                xl[i % 2][:, cols], xw[i % 2][:, cols], xh[i % 2][:, cols].bitcast(F32), ALU.subtract),
                f"xl{i}.{h}", [f"xh{i}.{h}"])

    def load_g(h, k):
        dma("sync", f"wb{k}", gw[k], g_raw[k, :, h * H:(h + 1) * H], f"g{NB * h + k}",
            [f"k{NT - 1}.{k}"] if h else [f"slice{k}", f"sg{5 * k + 2}", f"sg{5 * k + 1}"])

    def split_g(h, k):
        n = NB * h + k
        op("scalar", lambda e: e.activation(gh[k], gw[k], ACT.Copy), f"gh{n}", [f"g{n}"])
        op("vector", lambda e: e.tensor_tensor(gl[k], gw[k], gh[k].bitcast(F32), ALU.subtract), f"gl{n}",
           [f"gh{n}"])

    def prepare_low():
        op("vector", lambda e: e.memset(raw, 0.0), "raw0", ["pg69"])
        for k in (0, 32, 64):
            dma("sync", f"bw{k}", raw[k:k + NR, :], io["bw"], f"bw{k}", ["raw0"])
        for k in (0, 64):
            dma("sync", f"bb{k}", raw[k + NR:k + NR + 1, :], io["b"], f"bb{k}", ["raw0"])
        op("scalar", lambda e: e.activation(bs, raw[0:96, :], ACT.Copy), "bs.hi",
           ["bw0", "bw32", "bw64", "bb0", "bb64", "sg73", "sg74", f"pd{B}.3"])
        op("vector", lambda e: e.tensor_tensor(bs[64:96, :], raw[64:96, :], bs[64:96, :].bitcast(F32), ALU.subtract),
           "bs", ["bs.hi"])
        op("vector", lambda e: e.memset(cr, 0.0), "cr0", [last_we])
        for k in (0, 32, 64):
            dma("sync", f"cr{k}", cr[:, k:k + NR], io["cores"], f"cr.{k}", ["cr0"])
        dma("sync", "se", se, io["se"], "se", [last_we])
        op("gpsimd", lambda e: e.memset(rr.bitcast(F32), 0.0), "rr0", [f"pp{B}.{NP - 1}.1"])
        for t in range(NT):
            op("gpsimd", lambda e, t=t: e.memset(sa[t].bitcast(F32), 1.0), f"s1.{t}",
               [f"s0.{t - 1}"] if t else [f"q{B}"])
            op("gpsimd", lambda e, t=t: e.memset(sa[t][32:64, :].bitcast(F32), 0.0), f"s0.{t}", [f"s1.{t}"])

    def split_r(k0, k1, after):
        op("scalar", lambda e: e.activation(rr[:, k0:k1, 0:XW], r_raw[:, k0:k1, :], ACT.Copy), f"rh{k1}", after)
        op("vector", lambda e: e.tensor_tensor(
            rr[:, k0:k1, XW:2 * XW], r_raw[:, k0:k1, :], rr[:, k0:k1, 0:XW].bitcast(F32), ALU.subtract),
            f"rr{k1}", [f"rh{k1}"])

    def finish_last():
        done = f"pg{5 * B + 4}"
        op("scalar", lambda e: e.activation(r_raw[:, B, :], pm[:, CUT[5] - XW - CUT[4]:CUT[5] - CUT[4]], ACT.Copy),
           f"re{B}", [done])
        for c in range(3):
            c0, c1 = CUT[c], min(CUT[c + 1], H)
            op("scalar", lambda e, c=c, c0=c0, c1=c1: e.activation(
                gh[B][:, c0:c1], po[c][:, 0:c1 - c0], ACT.Copy), f"gh{B}.{c}", [done])
            op("vector", lambda e, c=c, c0=c0, c1=c1: e.tensor_tensor(
                gl[B][:, c0:c1], po[c][:, 0:c1 - c0], gh[B][:, c0:c1].bitcast(F32), ALU.subtract),
                f"gl{B}" if c == 2 else f"gl{B}.{c}", [f"gh{B}.{c}"])
        split_r(B, NB, [f"re{B}"])
        for c in (3, 4, 2):
            c0, c1 = max(CUT[c], H), min(CUT[c + 1], D)
            src = po[c] if c < 4 else pm
            op("scalar", lambda e, c=c, c0=c0, c1=c1, src=src: e.activation(
                room.last[:, c0 - H:c1 - H], src[:, c0 - CUT[c]:c1 - CUT[c]], ACT.Copy), f"ge{5 * B + c}", [done, f"gl{B}"])
        dma("sync", "sgl", g_raw[B, :, H:D], room.last, "sg.last", [f"ge{5 * B + c}" for c in (2, 3, 4)])

    def xs(x, k):
        return x[:, k * 128:(k + 1) * 128]

    def route_pe(i, k):
        for n, x in enumerate((xh[i % 2], xl[i % 2])):
            after = []
            if n == 0 and k in (0, NB // 2):
                after = [f"xl{i}.{k // (NB // 2)}", f"rr{NB}"] + ([f"pj{i - 1}"] if i else [])
            op("tensor", lambda e, x=x, n=n: e.matmul(
                pp[0:XM, 0:128], rr[:, k, :], xs(x, k), start=k == 0 and n == 0, stop=k == NB - 1 and n == 1),
                f"pp{i}" if k == NB - 1 and n else None, after)

    def proj_act(i):
        op("scalar", lambda e: e.activation(pj, pp[0:2 * XW, 0:128], ACT.Copy), f"pj{i}",
           [f"pp{i}"] + ([f"ps{i - 1}"] if i else []))

    def proj_pe(i):
        op("tensor", lambda e: e.matmul(ps[:, 0:XW], pj, se, start=True, stop=True), f"ps{i}",
           [f"pj{i}", "se"] + ([f"z{i - 1}"] if i else []))

    def route_chain(i):
        lg = ps[:, NR:XW]
        op("vector", lambda e: e.tensor_reduce(st[:, 0:1], lg, AXX, ALU.max), f"mx{i}", [f"ps{i}"])
        op("vector", lambda e: e.tensor_scalar(st[:, 1:2], st[:, 0:1], -1.0, None, ALU.mult), f"nm{i}", [f"mx{i}"])
        op("scalar", lambda e: e.activation(ex, lg, ACT.Exp, bias=st[:, 1:2], scale=1.0), f"ex{i}", [f"nm{i}"])
        op("vector", lambda e: e.tensor_reduce(st[:, 2:3], ex, AXX, ALU.add), f"sm{i}", [f"ex{i}"])
        op("vector", lambda e: e.reciprocal(st[:, 3:4], st[:, 2:3]), f"rc{i}", [f"sm{i}"])
        op("vector", lambda e: e.tensor_scalar(pe_, ex, st[:, 3:4], 2.0, ALU.mult, ALU.mult), f"pr{i}", [f"rc{i}"])
        op("vector", lambda e: e.tensor_tensor(
            z.rearrange("p (a r) -> p a r", a=NE), pe_.unsqueeze(2).to_broadcast([128, NE, NR]),
            ps[:, 0:NR].unsqueeze(1).to_broadcast([128, NE, NR]), ALU.mult), f"z{i}",
            [f"pr{i}"] + ([f"pm{i - 1}"] if i else []))

    def turn_pe(i):
        op("tensor", lambda e: e.transpose(pz[:, 0:128], z, idn), f"pz{i}",
           [f"z{i}", "id"] + ([f"zt{i - 1}"] if i else ["ge74"]))

    def turn_act(i):
        op("scalar", lambda e: e.activation(zt, pz[:, 0:128], ACT.Copy), f"zt{i}",
           [f"pz{i}"] + ([f"pm{i - 1}"] if i else []))

    def mix_pe(i):
        op("tensor", lambda e: e.matmul(pm[0:96, 0:128], cr, zt, start=True, stop=True), f"pm{i}",
           [f"zt{i}", "cr.0", "cr.32", "cr.64"] + ([f"ml{i - 1}"] if i else [f"ge{5 * B + 4}"]))

    def mix_out(i):
        for k in (0, 32, 64):
            op("scalar", lambda e, k=k: e.activation(sa[i][k:k + NR, :], pm[k:k + NR, 0:128], ACT.Copy),
               f"mh{i}.{k}", [f"pm{i}", f"s0.{i}"])
        op("vector", lambda e: e.tensor_tensor(sa[i][32:32 + NR, :], pm[32:32 + NR, 0:128],
                                               sa[i][32:32 + NR, :].bitcast(F32), ALU.subtract),
           f"ml{i}", [f"mh{i}.64"])

    def main_pe(i, k):
        h = i // NT
        n = 0
        for x, w in ((xh[i % 2], gh), (xh[i % 2], gl), (xl[i % 2], gh)):
            for c in range(2):
                n += 1
                after = [f"gl{NB * h + k}"] if n == 1 else []
                if n == 1 and k % (NB // 2) == 0:
                    after.append(f"xl{kept(i)}.{k // (NB // 2)}")
                if k == 0 and n <= 2:
                    if i >= 2:
                        after.append(f"o{i - 2}.{c}")
                    elif i == 0:
                        after.append(f"gl{B}.{c}")
                    else:
                        after.append(f"ge{5 * B + 2 + c}")
                        if c == 0:
                            after.append(f"gl{B}")
                op("tensor", lambda e, x=x, w=w, c=c, n=n: e.matmul(
                    po[2 * (i % 2) + c], xs(x, k), w[k][:, c * 512:(c + 1) * 512],
                    start=k == 0 and n <= 2, stop=False),
                    f"k{i}.{k}" if n == 6 and i == NT - 1 else None, after)

    def low_pe(i):
        h, t = tiles[i]
        for c in range(2):
            op("tensor", lambda e, c=c: e.matmul(
                po[2 * (i % 2) + c], sa[t], bs[:, h * H + c * 512:h * H + (c + 1) * 512],
                start=False, stop=True), f"pt{i}" if c else f"pt{i}.0", [f"ml{t}", "bs"])

    def evacuate(i):
        for c, engine in enumerate(("scalar", "vector")):
            after = [f"pt{i}"] + ([f"st{i - 2}.{c}"] if i >= 2 else ["sg.last"] if i else [f"pg{5 * B + 4}"])
            dst, src = os_[2 * (i % 2) + c], po[2 * (i % 2) + c]
            if c == 0:
                op(engine, lambda e, dst=dst, src=src: e.activation(dst, src, ACT.Copy), f"o{i}.0", after)
            else:
                op(engine, lambda e, dst=dst, src=src: e.tensor_copy(dst, src), f"o{i}.1", after)

    def store(i):
        h, t = tiles[i]
        for c in range(2):
            n = 2 * (i % 2) + c
            dma("sync", f"st{n}", out[t, :, h * H + c * 512:h * H + (c + 1) * 512], os_[n], f"st{i}.{c}",
                [f"o{i}.{c}"])

    def tail_pe(i, k):
        if i >= NT:
            return
        if i == 0 and 1 <= k <= 8:
            route_pe(0, 2 * k - 2)
            route_pe(0, 2 * k - 1)
        hops = {10: proj_pe, 12: turn_pe, 15: mix_pe} if i == 0 else {2: proj_pe, 6: turn_pe, 11: mix_pe}
        if k in hops:
            hops[k](i)
        if i + 1 < NT and k == 13:
            for kk in range(NB):
                route_pe(i + 1, kk)

    load_x(0)
    split(0)
    prepare_low()
    split_r(0, B, ["rr0", f"re{B - 1}"])
    load_x(1)
    for k in range(B):
        load_g(0, k)
        split_g(0, k)
    finish_last()
    for i in range(N):
        for k in range(NB):
            main_pe(i, k)
            tail_pe(i, k)
        low_pe(i)
        fresh = i + 1 < N and kept(i + 1) == i + 1
        if i:
            if fresh:
                load_x(i + 1)
            evacuate(i - 1)
            store(i - 1)
        else:
            split(1)
        if i < NT:
            proj_act(i)
            route_chain(i)
        if fresh and i:
            split(i + 1)
        if i < NT:
            turn_act(i)
            mix_out(i)
        if i == NT - 1:
            for k in range(NB):
                load_g(1, k)
                split_g(1, k)
    evacuate(N - 1)
    store(N - 1)
    ends = [f"st{i}.{c}" for i in (N - 2, N - 1) for c in range(2)]
    pl.end("sync", ends)


def build(nc, io, out):
    g_raw = nc.dram_tensor("g_raw", [NB, 128, D], F32, kind="Internal").ap()
    with ExitStack() as ctx:
        plan = Plan(nc, ctx)
        room = Room(nc, ctx)
        plan_weights(plan, room, io, g_raw)
        plan_tokens(plan, room, io, g_raw, out)
        run_block(nc, plan)


def kernel(x, condB_codebook, L0_cond_weight, L0_cond_scale_log, L0_cond_lora_A, L0_cond_lora_B, L0_ffn_W_base,
           L0_ffn_b_base, L0_ffn_A_w, L0_ffn_B_w, L0_ffn_router_w, L0_ffn_cores):
    import concourse.bacc as bacc
    from concourse.bass_utils import run_bass_kernel_spmd

    def lay(a):
        return np.ascontiguousarray(a)

    x = np.asarray(x)
    wide = np.concatenate([np.asarray(L0_ffn_W_base), np.asarray(L0_ffn_A_w), np.asarray(L0_ffn_router_w)], axis=0)
    la = np.asarray(L0_cond_lora_A)
    arrays = {
        "x": lay(x.reshape(NT, 128, NB, 128).transpose(0, 3, 2, 1).reshape(NT, 128, D)),
        "w": lay(np.asarray(L0_cond_weight).reshape(NB, 128, NB, 128).transpose(2, 1, 0, 3).reshape(NB, 128, D)),
        "sl": lay(np.asarray(L0_cond_scale_log).reshape(NB, 128, NB).transpose(1, 2, 0).reshape(128, NB * NB)),
        "lb": lay(np.asarray(L0_cond_lora_B).reshape(2, 1024, 64).transpose(0, 2, 1).reshape(128, 1024)),
        "la": lay(np.concatenate([la, la], axis=0)),
        "wb": lay(wide.T.reshape(NB, 128, DX)),
        "cores": lay(np.asarray(L0_ffn_cores).reshape(128, NR)),
        "bw": lay(np.asarray(L0_ffn_B_w).T),
        "b": lay(np.asarray(L0_ffn_b_base).reshape(1, D)),
        "cb": lay(np.asarray(condB_codebook)),
        "id": np.eye(128, dtype=np.float32),
        "se": np.tile(np.eye(XW, dtype=np.float32), (2, 1)),
    }
    nc = bacc.Bacc("TRN2", target_bir_lowering=False, num_devices=1)
    io = {k: nc.dram_tensor(f"in_{k}", a.shape, F32, kind="ExternalInput").ap() for k, a in arrays.items()}
    out = nc.dram_tensor("out", [NT, 128, D], F32, kind="ExternalOutput").ap()
    build(nc, io, out)
    r = run_bass_kernel_spmd(nc, [{f"in_{k}": a for k, a in arrays.items()}], core_ids=[0])
    return r.results[0]["out"].reshape(32, 128, D)
```

```python
import numpy as np
from contextlib import ExitStack

import concourse.bass as bass
import concourse.mybir as mybir

F32 = mybir.dt.float32
F32R = mybir.dt.float32r
I32 = mybir.dt.int32
U8 = mybir.dt.uint8
ALU = mybir.AluOpType
ACT = mybir.ActivationFunctionType
AXX = mybir.AxisListType.X

D = 2048
NB = 16
NT = 32
NE = 8
NR = 16
XW = NE + NR
DX = D + XW
NC = 32
NJ = NC - 1
NP = 6
NM = 3
NW = 3
SPARE_AT = (0, 3, 9, 13, 17, 21)
DELTA_AT = (5, 6, 8, 9)
PART_AT = (12, 16, 19, 24)
CUT = (0, 384, 768, 1152, 1664, DX)
NV = NJ - NP
HX = D // 2 + XW
CUT_TOKENS = ((0, 352, 704, HX), (0, 512, D // 2))
GROW = float(2.0 ** 100)
FULL = 255.0


class Plan:

    def __init__(self, nc, ctx):
        self.nc, self.ctx = nc, ctx
        self.lines = {e: [] for e in ("sync", "scalar", "vector", "gpsimd", "tensor")}
        self.sems, self.count, self.at = {}, {}, {}

    def _sem(self, key):
        if key not in self.sems:
            self.sems[key] = self.ctx.enter_context(self.nc.semaphore(f"s_{key}"))
            self.count[key] = 0
        return self.sems[key]

    def op(self, engine, fn, name=None, after=()):
        if name is not None:
            self._sem(engine)
            self.count[engine] += 1
            assert name not in self.at, name
            self.at[name] = (engine, self.count[engine])
        self.lines[engine].append((fn, tuple(after), (engine, 1) if name is not None else None))

    def dma(self, engine, slot, out, src, name, after=()):
        key = f"d_{slot}"
        self._sem(key)
        self.count[key] += 16
        assert name not in self.at, name
        self.at[name] = (key, self.count[key])
        self.lines[engine].append((lambda e: e.dma_start(out, src), tuple(after), (key, 16)))

    def end(self, engine, names):
        self.lines[engine].append((None, tuple(names), None))

    def emit(self, engine, eng):
        seen = {}
        for fn, after, sig in self.lines[engine]:
            for w in after:
                key, n = self.at[w]
                if seen.get(key, 0) < n:
                    seen[key] = n
                    eng.wait_ge(self.sems[key], n)
            if fn is None:
                continue
            inst = fn(eng)
            if sig is not None:
                inst.then_inc(self.sems[sig[0]], sig[1])


def run_block(nc, plan):
    with nc.Block() as block:
        @block.sync
        def _(e):
            plan.emit("sync", e)

        @block.scalar
        def _(e):
            plan.emit("scalar", e)

        @block.vector
        def _(e):
            plan.emit("vector", e)

        @block.gpsimd
        def _(e):
            plan.emit("gpsimd", e)

        @block.tensor
        def _(e):
            plan.emit("tensor", e)


class Room:

    def __init__(self, nc, ctx):
        self.nc = nc
        self.top = self.low = -(-nc.sbuf_base // 32) * 32
        H = D // 2
        at_wb = self.top
        self.wb = [self.take(f"wb{k}", DX) for k in range(NB)]
        at_nt = self.top
        self.nt = [self.take(f"nt{k}", D) for k in range(NW)]
        at_dl = self.top
        self.dl = [self.take(f"dl{k}", D) for k in range(2)]
        at_pp = self.top
        self.pp = self.take("pp", D)
        self.mk = [self.take(f"mk{k}", D, U8) for k in range(NM)]
        self.mp = [self.take(f"mp{k}", D, U8) for k in range(2)]
        self.tm = self.take("tm", H)
        at_gs = self.top
        self.gs = [self.take(f"gs{k}", 512) for k in range(2)]
        self.lb = self.take("lb", H)
        at_la = self.top
        self.la = [self.take(f"la{k}", 128) for k in range(2)]
        at_sc = self.top
        self.sc = self.take("sc", NB * NB)
        self.rs = self.take("rs", NB * NB)
        self.idn = self.take("idn", 128)
        self.cb = self.take("cb", NC)
        self.cn = self.take("cn", NC)
        self.u = self.take("u", NC + 1)
        self.th = self.take("th", NJ)
        self.bj = self.take("bj", NJ)
        self.dj = self.take("dj", NJ)
        self.sm = self.take("sm", 2)
        self.r_raw = self.take("r_raw", NB * XW).rearrange("p (k r) -> p k r", k=NB)

        self.gh, self.gw, self.gl = [], [], []
        for k in range(NB):
            at = at_wb + k * HX * 8
            self.gh.append(self.put(f"gh{k}", at, HX, F32R))
            self.gw.append(self.put(f"gw{k}", at + HX * 4, HX))
            self.gl.append(self.put(f"gl{k}", at + HX * 4, HX, F32R))
        assert at_wb + NB * HX * 8 <= at_nt + H * 4
        self.last = self.put("last", at_nt + H * 4, H)
        self.os = [self.put("os0", at_nt + H * 4, H), self.put("os1", at_pp + NT * 512, H)]
        assert at_pp + NT * 512 + H * 4 <= at_gs
        at_x = [(at_dl + D * 4, at_dl), (at_nt + D * 4, at_nt + 2 * D * 4)]
        self.xh = [self.put(f"xh{k}", a, D, F32R) for k, (a, _) in enumerate(at_x)]
        self.xw = [self.put(f"xw{k}", a, D) for k, (_, a) in enumerate(at_x)]
        self.xl = [self.put(f"xl{k}", a, D, F32R) for k, (_, a) in enumerate(at_x)]
        self.bw = self.put("bw", at_nt + D * 4, D)
        self.sa = [self.put(f"sa{k}", at_pp + k * 512, 128, F32R, 96) for k in range(NT)]
        self.bs = self.put("bs", at_gs, D, F32R, 96)
        self.z = self.put("z", at_la + 512, 128)
        self.cr = self.put("cr", at_sc, 96)
        self.ex = self.put("ex", at_sc + 512, NE)
        self.pe = self.put("pe", at_sc + 544, NE)
        self.st = self.put("st", at_sc + 576, 4)

        def bank(name, n):
            return ctx.enter_context(nc.psum_tensor(name, [128, n * 512], F32))[:]

        self.acc = bank("acc", 4)
        self.pg = [bank(f"pg{k}", 1) for k in range(2)]
        self.pd = [bank(f"pd{k}", 1) for k in range(2)]
        self.po = [self.acc[:, k * 512:(k + 1) * 512] for k in range(4)]

    def put(self, name, at, n, dtype=F32, rows=128):
        return self.nc.alloc_sbuf_tensor_at(name, [rows, n], dtype, offset=at)[:]

    def take(self, name, n, dtype=F32):
        at = self.top
        self.top += -(-n * (1 if dtype is U8 else 4) // 32) * 32
        return self.put(name, at, n, dtype)


def plan_weights(pl, room, io, g_raw):
    op, dma = pl.op, pl.dma
    wb, nt, dl, pp, mk, mp, tm, gs, lb, la = (room.wb, room.nt, room.dl, room.pp, room.mk, room.mp, room.tm, room.gs,
                                              room.lb, room.la)
    sc, rs, idn, cb, cn, u, th, bj, dj, sm = (room.sc, room.rs, room.idn, room.cb, room.cn, room.u, room.th, room.bj,
                                              room.dj, room.sm)
    r_raw, acc, pg, pd = room.r_raw, room.acc, room.pg, room.pd

    s = pp[:, 0:256]
    kf = pp[:, 256:512]
    r = pp[:, 512:768]
    p2 = pp[:, 768:1024]
    k1 = pp[:, 1024:1280].bitcast(I32)
    k2 = pp[:, 1280:1536].bitcast(I32)

    dma("sync", "sl", sc, io["sl"], "sl")
    dma("sync", "lb", lb, io["lb"], "lb")
    dma("sync", "la0", la[0], io["la"][:, 0:128], "la0")
    dma("sync", "cb", cb, io["cb"].partition_broadcast(128), "cb")
    dma("sync", "w0", nt[0], io["w"][0], "w0")
    dma("sync", "la1", la[1], io["la"][:, 128:256], "la1")
    for b in range(1, NW):
        dma("sync", f"w{b}", nt[b], io["w"][b], f"w{b}")
    dma("sync", "id", idn, io["id"], "id")
    for t in range(NB):
        dma("sync", f"wb{t}", wb[t], io["wb"][t], f"wb{t}")

    chains = {"es": [], "bk": []}

    def step(chain, fn, after=()):
        steps = chains[chain]
        steps.append((fn, after))
        return f"{chain}{len(steps) - 1}"

    def v(fn, after=()):
        return step("es", fn, after)

    def w(fn, after=()):
        return step("bk", fn, after)

    LOG2E, LN2H, LN2L = 1.4426950408889634, 0.693359375, -2.12194440054690581e-4
    v(lambda e: e.tensor_scalar(s, sc, 100.0, -110.0, ALU.min, ALU.max), ("sl",))
    v(lambda e: e.tensor_scalar(k2, s, LOG2E, None, ALU.mult))
    v(lambda e: e.tensor_copy(kf, k2))
    v(lambda e: e.scalar_tensor_tensor(r, kf, -LN2H, s, ALU.mult, ALU.add))
    v(lambda e: e.scalar_tensor_tensor(r, kf, -LN2L, r, ALU.mult, ALU.add))
    co = [1.0 / 40320, 1.0 / 5040, 1.0 / 720, 1.0 / 120, 1.0 / 24, 1.0 / 6, 0.5, 1.0, 1.0]
    v(lambda e: e.tensor_scalar(p2, r, co[0], co[1], ALU.mult, ALU.add))
    for c in co[2:]:
        v(lambda e: e.tensor_tensor(p2, p2, r, ALU.mult))
        v(lambda e, c=c: e.tensor_scalar(p2, p2, c, None, ALU.add))
    v(lambda e: e.tensor_scalar(k1, k2, 1, None, ALU.arith_shift_right))
    v(lambda e: e.tensor_tensor(k2, k2, k1, ALU.subtract))
    for k in (k1, k2):
        v(lambda e, k=k: e.tensor_scalar(k, k, 127.0, None, ALU.add))
        v(lambda e, k=k: e.tensor_scalar(k, k, 23, None, ALU.logical_shift_left))
    v(lambda e: e.tensor_tensor(p2, p2, pp[:, 1024:1280], ALU.mult))
    v(lambda e: e.tensor_tensor(sc, p2, pp[:, 1280:1536], ALU.mult))
    scale_first = v(lambda e: e.reciprocal(rs[:, 0:NB], sc[:, 0:NB]))
    scale_ready = v(lambda e: e.reciprocal(rs[:, NB:], sc[:, NB:]))

    w(lambda e: e.tensor_scalar(cn, cb, -1.0, None, ALU.mult), ("cb",))
    w(lambda e: e.tensor_tensor(cn, cn, cb, ALU.max))
    w(lambda e: e.tensor_reduce(sm[:, 0:1], cn, AXX, ALU.max))
    w(lambda e: e.tensor_scalar(sm[:, 0:1], sm[:, 0:1], 1e-8, None, ALU.max))
    w(lambda e: e.reciprocal(sm[:, 1:2], sm[:, 0:1]))
    w(lambda e: e.tensor_scalar(cn, cb, sm[:, 1:2], None, ALU.mult))
    w(lambda e: e.tensor_tensor(th, cn[:, 0:NJ], cn[:, 1:NC], ALU.add))
    w(lambda e: e.tensor_scalar(th, th, 0.5, None, ALU.mult))
    w(lambda e: e.tensor_tensor(dj, cn[:, 1:NC], cn[:, 0:NJ], ALU.subtract))
    w(lambda e: e.tensor_scalar(dj, dj, 1.0 / FULL, None, ALU.mult))
    w(lambda e: e.memset(u[:, 0:1], -3e38))
    w(lambda e: e.memset(u[:, NC:NC + 1], 3e38))
    for g in (16, 8, 4, 2, 1):
        n = NC // (2 * g)
        e0, e1 = g, g + 2 * g * (n - 1) + 1
        w(lambda e, g=g, e0=e0, e1=e1: e.tensor_tensor(
            u[:, e0:e1:2 * g], th[:, e0 - 1:e1 - 1:2 * g], u[:, e0 - g:e1 - g:2 * g], ALU.max))
        w(lambda e, g=g, e0=e0, e1=e1: e.tensor_tensor(
            u[:, e0:e1:2 * g], u[:, e0:e1:2 * g], u[:, e0 + g:e1 + g:2 * g], ALU.min))
    book_ready = w(lambda e: e.tensor_scalar(bj, u[:, 1:NC], -GROW, None, ALU.mult))
    for k in range(max(len(steps) for steps in chains.values())):
        for chain, steps in chains.items():
            if k < len(steps):
                fn, after = steps[k]
                op("vector", fn, f"{chain}{k}", (*after, *([f"{chain}{k - 1}"] if k else [])))

    def grouped(t):
        return t.rearrange("p (a i) -> p a i", a=NB)

    def per_group(t, b):
        return t[:, b * NB:(b + 1) * NB].unsqueeze(2).to_broadcast([128, NB, 128])

    def delta_pe(b, q):
        n = 4 * b + q
        for k in range(4):
            ot = 4 * q + k
            h = 64 * (ot // 8)
            after = []
            if k == 0:
                after = ["lb", f"la{b}"] + ([f"dl{(n - 2) // 4}.{(n - 2) % 4}"] if n >= 2 else [])
            op("tensor", lambda e, k=k, ot=ot, h=h: e.matmul(
                pd[n % 2][:, k * 128:(k + 1) * 128], lb[h:h + 64, (ot % 8) * 128:(ot % 8 + 1) * 128],
                la[b % 2][h:h + 64, :], start=True, stop=True),
                f"pd{b}.{q}" if k == 3 else None, after)

    def delta_act(b, q):
        op("scalar", lambda e: e.activation(
            dl[b % 2][:, q * 512:(q + 1) * 512], pd[(4 * b + q) % 2], ACT.Copy, scale=0.5), f"dl{b}.{q}",
           [f"pd{b}.{q}"] + ([f"we{b - 2}"] if b >= 2 else []))

    def normalise(b):
        for q in range(4 if b == 0 else 1):
            cols = slice(q * 512, (q + 1) * 512) if b == 0 else slice(0, D)
            op("gpsimd", lambda e, cols=cols: e.tensor_tensor(
                nt[b % NW][:, cols], nt[b % NW][:, cols], dl[b % 2][:, cols], ALU.add),
               f"wg{b}" if q == 3 or b else f"wg{b}.{q}", [f"w{b}", f"dl{b}.{3 if b else q}"])
        op("gpsimd", lambda e: e.tensor_tensor(grouped(nt[b % NW]), grouped(nt[b % NW]),
                                               per_group(rs, b), ALU.mult),
           f"n{b}", [f"wg{b}", scale_ready if b else scale_first])

    HD = D // 2

    def spare_mask(b, i):
        k = NP * b + i
        after = [f"n{b}", book_ready]
        if k >= 2:
            after.append(f"pp{(k - 2) // NP}.{(k - 2) % NP}.1")
        op("scalar", lambda e: e.activation(mp[k % 2], nt[b % NW], ACT.Identity,
                                            bias=bj[:, NV + i:NV + i + 1], scale=GROW), f"mp{b}.{i}", after)

    def spare(b, i):
        k, j = NP * b + i, NV + i
        for h in range(2):
            cols = slice(h * HD, (h + 1) * HD)
            after = [f"mp{b}.{i}", book_ready]
            if k or h:
                kk = 2 * k + h - 1
                after.append(f"pp{kk // 2 // NP}.{kk // 2 % NP}.{kk % 2}")
            op("gpsimd", lambda e, cols=cols: e.tensor_scalar(
                tm, mp[k % 2][:, cols], dj[:, j:j + 1], 0.0, ALU.mult, ALU.add), f"tm{b}.{i}.{h}", after)
            src = pp if i else nt[b % NW]
            op("gpsimd", lambda e, cols=cols: e.tensor_tensor(pp[:, cols], src[:, cols], tm, ALU.add),
               f"pp{b}.{i}.{h}", [f"tm{b}.{i}.{h}"] + ([f"q{b - 1}"] if b and i == 0 else []))

    def mask(b, j):
        k = NV * b + j
        after = [f"n{b}", book_ready]
        if k >= NM:
            after.append(f"ac{(k - NM) // NV}.{(k - NM) % NV}.1")
        op("scalar", lambda e: e.activation(mk[k % NM], nt[b % NW], ACT.Identity,
                                            bias=bj[:, j:j + 1], scale=GROW), f"mk{b}.{j}", after)

    def add(b, j):
        k = NV * b + j
        for h in range(2):
            cols = slice(h * HD, (h + 1) * HD)
            if j == 0:
                op("vector", lambda e, cols=cols: e.scalar_tensor_tensor(
                    acc[:, cols], mk[k % NM][:, cols], dj[:, 0:1], nt[b % NW][:, cols], ALU.mult, ALU.subtract),
                    f"ac{b}.0.{h}", [f"mk{b}.0"] + ([f"q{b - 1}"] if b else []))
            else:
                op("vector", lambda e, cols=cols: e.scalar_tensor_tensor(
                    acc[:, cols], mk[k % NM][:, cols], dj[:, j:j + 1], acc[:, cols], ALU.mult, ALU.add),
                    f"ac{b}.{j}.{h}", [f"mk{b}.{j}", f"ac{b}.{j - 1}.{h}"])

    def close(b):
        op("vector", lambda e: e.scalar_tensor_tensor(
            nt[b % NW], acc, cn[:, 0:1], pp, ALU.add, ALU.add), f"q{b}",
           [f"ac{b}.{NV - 1}.1", f"mk{b}.{NV - 1}", f"pp{b}.{NP - 1}.1"])

    def effective(b):
        op("gpsimd", lambda e: e.tensor_tensor(grouped(nt[b % NW]), grouped(nt[b % NW]), per_group(sc, b), ALU.mult),
           f"ws{b}", [f"q{b}"])
        op("gpsimd", lambda e: e.tensor_tensor(nt[b % NW], nt[b % NW], dl[b % 2], ALU.add), f"we{b}", [f"ws{b}"])

    def effective_last(b):
        for q in range(4):
            cols = slice(q * 512, (q + 1) * 512)
            op("gpsimd", lambda e, q=q, cols=cols: e.tensor_tensor(
                nt[b % NW][:, cols].rearrange("p (a i) -> p a i", a=4), nt[b % NW][:, cols].rearrange("p (a i) -> p a i", a=4),
                sc[:, b * NB + 4 * q:b * NB + 4 * q + 4].unsqueeze(2).to_broadcast([128, 4, 128]), ALU.mult),
                f"ws{b}.{q}", [f"q{b}"])
            op("gpsimd", lambda e, cols=cols: e.tensor_tensor(
                nt[b % NW][:, cols], nt[b % NW][:, cols], dl[b % 2][:, cols], ALU.add), f"we{b}.{q}", [f"ws{b}.{q}"])

    def product(b):
        for c in range(5):
            k = 5 * b + c
            c0, c1 = CUT[c], CUT[c + 1]
            out = pg[k % 2]
            own = c0 <= b * 128 < c1
            for t in range(NB):
                if b + 2 < NB and c == 0 and t in (5, 10):
                    delta_pe(b + 2, 2 + (t == 10))
                after = [f"wb{t}"]
                if t == 0:
                    after += [f"we{b}"] + ([f"ge{k - 2}"] if k >= 2 else [])
                end = t == NB - 1 and not own
                op("tensor", lambda e, t=t, out=out, c0=c0, c1=c1, end=end: e.matmul(
                    out[:, 0:c1 - c0], nt[b % NW][:, t * 128:(t + 1) * 128],
                    wb[t][:, c0:c1], start=t == 0, stop=end), f"pg{k}" if end else None, after)
            if own:
                o = b * 128 - c0
                op("tensor", lambda e, out=out, o=o: e.matmul(
                    out[:, o:o + 128], idn, idn, start=False, stop=True), f"pg{k}", ["id"])

    def product_last(b):
        for t in range(NB):
            for c in range(5):
                k = 5 * b + c
                c0, c1 = CUT[c], CUT[c + 1]
                out = room.po[c] if c < 4 else pg[k % 2]
                after = [f"we{b}.{t // 4}"] if t % 4 == 0 and c == 0 else []
                if c == 4 and t == 0:
                    after.append(f"ge{k - 6}")
                op("tensor", lambda e, t=t, out=out, c0=c0, c1=c1, c=c: e.matmul(
                    out[:, 0:c1 - c0], nt[b % NW][:, t * 128:(t + 1) * 128], wb[t][:, c0:c1],
                    start=t == 0, stop=t == NB - 1 and c < 4),
                    f"pg{k}" if t == NB - 1 and c < 4 else f"slice{t}" if c == 4 else None, after)
        o = b * 128 - CUT[4]
        op("tensor", lambda e: e.matmul(pg[k % 2][:, o:o + 128], idn, idn, start=False, stop=True), f"pg{k}")

    def part_act(b, c):
        k = 5 * b + c
        n = min(CUT[c + 1], D) - CUT[c]
        if c == 4:
            op("scalar", lambda e: e.activation(r_raw[:, b, :], pg[k % 2][:, n:n + XW], ACT.Copy), f"re{b}",
               [f"pg{k}"])
        op("scalar", lambda e: e.activation(gs[k % 2][:, 0:n], pg[k % 2][:, 0:n], ACT.Copy), f"ge{k}",
           [f"pg{k}"] + ([f"sg{k - 2}"] if k >= 2 else []))

    def part_out(b, c):
        k = 5 * b + c
        c0, c1 = CUT[c], min(CUT[c + 1], D)
        dma("sync", f"sg{k % 2}", g_raw[b, :, c0:c1], gs[k % 2][:, 0:c1 - c0], f"sg{k}", [f"ge{k}"])

    for b in range(2):
        for q in range(4):
            delta_pe(b, q)
    for b in range(NB):
        if b + 2 < NB:
            delta_pe(b + 2, 0)
            delta_pe(b + 2, 1)
        if b + 1 < NB:
            product(b)
    product_last(NB - 1)

    for b in range(2):
        for q in range(4):
            delta_act(b, q)
    normalise(0)
    normalise(1)
    for b in range(NB):
        for j in range(NV):
            if j == 4 and b >= 2:
                part_act(b - 2, 4)
            if j in DELTA_AT and 2 <= b + 1 < NB:
                delta_act(b + 1, DELTA_AT.index(j))
            if b >= 1 and j in PART_AT:
                part_act(b - 1, PART_AT.index(j))
            mask(b, j)
            if j in SPARE_AT:
                spare_mask(b, SPARE_AT.index(j))
            add(b, j)
        close(b)
    part_act(NB - 2, 4)

    for b in range(NB):
        if b:
            effective(b - 1)
        for i in range(NP):
            if i == 2 and 1 <= b < NB - 1:
                normalise(b + 1)
            spare(b, i)
    effective_last(NB - 1)

    for b in range(NB):
        if b >= 2:
            part_out(b - 2, 4)
        if b >= 1:
            for c in range(4):
                part_out(b - 1, c)
        if b + 2 < NB:
            dma("sync", f"la{b % 2}", la[b % 2], io["la"][:, (b + 2) * 128:(b + 3) * 128], f"la{b + 2}",
                [f"pd{b}.3"])
        if b >= 1 and b + 2 < NB:
            dma("sync", f"w{(b - 1) % NW}", nt[(b - 1) % NW], io["w"][b + 2], f"w{b + 2}", [f"pg{5 * b - 1}"])
    part_out(NB - 2, 4)


def plan_tokens(pl, room, io, g_raw, out):
    op, dma = pl.op, pl.dma
    H = D // 2
    gh, gl, gw, xh, xl, xw, bs, sa, os_ = (room.gh, room.gl, room.gw, room.xh, room.xl, room.xw, room.bs, room.sa,
                                           room.os)
    idn, cr, ex, pe_, st, z, zt = room.idn, room.cr, room.ex, room.pe, room.st, room.z, room.z
    r_raw, raw, acc = room.r_raw, room.bw, room.po
    po, pz, pm = (acc[0:3], (acc[3], *room.pd)), room.pg[0], room.pg[1]
    B = NB - 1
    last_we = f"we{B}.3"
    tiles = [(0, t) for t in range(NT)] + [(1, t) for t in (NT - 2, NT - 1, *range(NT - 2))]
    N = len(tiles)

    def kept(i):
        return i - 2 if i in (NT, NT + 1) else i

    def chunks(i):
        cuts = CUT_TOKENS[tiles[i][0]]
        return [(c0, c1, min(c1, H), bank) for c0, c1, bank in zip(cuts, cuts[1:], po[i % 2])]

    def used(i):
        return f"mn{i}" if i < NT else f"pt{i}"

    def load_x(i):
        free = [used(i - 2)] if i >= 2 else ["we14"] if i == 0 else ["pg74"]
        for h in range(2):
            cols = slice(h * H, (h + 1) * H)
            dma("sync", f"x{i % 2}.{h}", xw[i % 2][:, cols], io["x"][tiles[i][1], :, cols], f"x{i}.{h}", free)

    def split(i):
        free = [used(i - 2)] if i >= 2 else [last_we] if i == 0 else ["bs"]
        for h in range(2):
            cols = slice(h * H, (h + 1) * H)
            op("scalar", lambda e, cols=cols: e.activation(xh[i % 2][:, cols], xw[i % 2][:, cols], ACT.Copy),
               f"xh{i}.{h}", [f"x{i}.{h}", *free])
            op("vector", lambda e, cols=cols: e.tensor_tensor(
                xl[i % 2][:, cols], xw[i % 2][:, cols], xh[i % 2][:, cols].bitcast(F32), ALU.subtract),
                f"xl{i}.{h}", [f"xh{i}.{h}"])

    def load_g(h, k):
        dma("sync", f"wb{k}", gw[k][:, 0:H], g_raw[k, :, h * H:(h + 1) * H], f"g{NB * h + k}",
            [f"k{NT - 1}.{k}" if k < B else used(NT - 1)] if h else
            [f"slice{k + 1}", f"sg{5 * k + 2}", f"sg{5 * k + 1}"])

    def split_g(h, k):
        n = NB * h + k
        cols = slice(0, H if h else HX)
        after = [f"g{n}"]
        if h == 0:
            op("gpsimd", lambda e: e.tensor_copy(gw[k][:, H:HX], r_raw[:, k, :]), f"rg{k}", [f"slice{k + 1}", f"re{k}", f"s0.{NT - 1}"])
            after.append(f"rg{k}")
        op("scalar", lambda e: e.activation(gh[k][:, cols], gw[k][:, cols], ACT.Copy), f"gh{n}", after)
        op("vector", lambda e: e.tensor_tensor(
            gl[k][:, cols], gw[k][:, cols], gh[k][:, cols].bitcast(F32), ALU.subtract), f"gl{n}", [f"gh{n}"])

    def prepare_low():
        op("vector", lambda e: e.memset(raw, 0.0), "raw0", ["pg69"])
        for k in (0, 32, 64):
            dma("sync", f"bw{k}", raw[k:k + NR, :], io["bw"], f"bw{k}", ["raw0"])
        for k in (0, 64):
            dma("sync", f"bb{k}", raw[k + NR:k + NR + 1, :], io["b"], f"bb{k}", ["raw0"])
        op("scalar", lambda e: e.activation(bs, raw[0:96, :], ACT.Copy), "bs.hi",
           ["bw0", "bw32", "bw64", "bb0", "bb64", "sg73", "sg74", f"pd{B}.3"])
        op("vector", lambda e: e.tensor_tensor(bs[64:96, :], raw[64:96, :], bs[64:96, :].bitcast(F32), ALU.subtract),
           "bs", ["bs.hi"])
        op("vector", lambda e: e.memset(cr, 0.0), "cr0", [last_we])
        for k in (0, 32, 64):
            dma("sync", f"cr{k}", cr[:, k:k + NR], io["cores"], f"cr.{k}", ["cr0"])
        for t in range(NT):
            op("gpsimd", lambda e, t=t: e.memset(sa[t].bitcast(F32), 1.0), f"s1.{t}",
               [f"s0.{t - 1}"] if t else [f"q{B}"])
            op("gpsimd", lambda e, t=t: e.memset(sa[t][32:64, :].bitcast(F32), 0.0), f"s0.{t}", [f"s1.{t}"])

    def finish_last():
        done = f"pg{5 * B + 4}"
        for c in range(3):
            c0, c1 = CUT[c], min(CUT[c + 1], H)
            op("scalar", lambda e, c=c, c0=c0, c1=c1: e.activation(
                gh[B][:, c0:c1], acc[c][:, 0:c1 - c0], ACT.Copy), f"gh{B}.{c}", [done])
            op("vector", lambda e, c=c, c0=c0, c1=c1: e.tensor_tensor(
                gl[B][:, c0:c1], acc[c][:, 0:c1 - c0], gh[B][:, c0:c1].bitcast(F32), ALU.subtract),
                f"gl{B}" if c == 2 else f"gl{B}.{c}", [f"gh{B}.{c}"])

        def keep(c, after):
            c0, c1 = max(CUT[c], H), min(CUT[c + 1], D)
            src = acc[c] if c < 4 else pm
            op("scalar", lambda e: e.activation(
                room.last[:, c0 - H:c1 - H], src[:, c0 - CUT[c]:c1 - CUT[c]], ACT.Copy), f"ge{5 * B + c}", [done, after])

        keep(3, done)
        keep(2, f"gl{B}")
        r0, r1 = D - CUT[4], DX - CUT[4]
        op("scalar", lambda e: e.activation(gh[B][:, H:HX], pm[:, r0:r1], ACT.Copy), f"rh{B}", [done])
        op("vector", lambda e: e.tensor_tensor(
            gl[B][:, H:HX], pm[:, r0:r1], gh[B][:, H:HX].bitcast(F32), ALU.subtract), f"rl{B}", [f"rh{B}"])
        keep(4, f"rl{B}")
        dma("sync", "sgl", g_raw[B, :, H:D], room.last, "sg.last", [f"ge{5 * B + c}" for c in (2, 3, 4)])

    def xs(x, k):
        return x[:, k * 128:(k + 1) * 128]

    def route_chain(i):
        c0, c1, r0, bank = chunks(i)[-1]
        ax, lg = bank[:, r0 - c0:r0 - c0 + NR], bank[:, r0 - c0 + NR:c1 - c0]
        op("vector", lambda e: e.tensor_reduce(st[:, 0:1], lg, AXX, ALU.max), f"mx{i}", [used(i)])
        op("vector", lambda e: e.tensor_scalar(st[:, 1:2], st[:, 0:1], -1.0, None, ALU.mult), f"nm{i}", [f"mx{i}"])
        op("scalar", lambda e: e.activation(ex, lg, ACT.Exp, bias=st[:, 1:2], scale=1.0), f"ex{i}", [f"nm{i}"])
        op("vector", lambda e: e.tensor_reduce(st[:, 2:3], ex, AXX, ALU.add), f"sm{i}", [f"ex{i}"])
        op("vector", lambda e: e.reciprocal(st[:, 3:4], st[:, 2:3]), f"rc{i}", [f"sm{i}"])
        op("vector", lambda e: e.tensor_scalar(pe_, ex, st[:, 3:4], 2.0, ALU.mult, ALU.mult), f"pr{i}", [f"rc{i}"])
        op("vector", lambda e: e.tensor_tensor(
            z.rearrange("p (a r) -> p a r", a=NE), pe_.unsqueeze(2).to_broadcast([128, NE, NR]),
            ax.unsqueeze(1).to_broadcast([128, NE, NR]), ALU.mult), f"z{i}",
            [f"pr{i}"] + ([f"pm{i - 1}"] if i else []))

    def turn_pe(i):
        op("tensor", lambda e: e.transpose(pz[:, 0:128], z, idn), f"pz{i}",
           [f"z{i}", "id"] + ([f"zt{i - 1}"] if i else ["ge74"]))

    def turn_act(i):
        op("scalar", lambda e: e.activation(zt, pz[:, 0:128], ACT.Copy), f"zt{i}",
           [f"pz{i}"] + ([f"pm{i - 1}"] if i else []))

    def mix_pe(i):
        op("tensor", lambda e: e.matmul(pm[0:96, 0:128], cr, zt, start=True, stop=True), f"pm{i}",
           [f"zt{i}", "cr.0", "cr.32", "cr.64"] + ([f"o{i - 1}.2"] if i else [f"ge{5 * B + 4}"]))

    def mix_out(i):
        for k in (0, 32, 64):
            op("scalar", lambda e, k=k: e.activation(sa[i][k:k + NR, :], pm[k:k + NR, 0:128], ACT.Copy),
               f"mh{i}.{k}", [f"pm{i}", f"s0.{i}"])
        op("vector", lambda e: e.tensor_tensor(sa[i][32:32 + NR, :], pm[32:32 + NR, 0:128],
                                               sa[i][32:32 + NR, :].bitcast(F32), ALU.subtract),
           f"ml{i}", [f"mh{i}.64"])

    def main_pe(i, k):
        h = i // NT
        parts = chunks(i)
        passes = ((xh[i % 2], gh), (xh[i % 2], gl), (xl[i % 2], gh))
        for n, (x, w) in enumerate(passes):
            for c, (c0, c1, _, bank) in enumerate(parts):
                after = []
                if n == c == 0:
                    after.append(f"gl{NB * h + k}")
                    if k % (NB // 2) == 0:
                        after.append(f"xl{kept(i)}.{k // (NB // 2)}")
                if n == k == 0:
                    if i >= 2:
                        after.append(f"o{i - 2}.{c}")
                    elif i == 0:
                        after.append(f"ge{5 * B + 2}" if c == 2 else f"gl{B}.{c}")
                    else:
                        after.append(f"dl{B}.{c + 1}" if c else f"ge{5 * B + 3}")
                if i == 0 and k == B and n == c == 0:
                    after.append(f"rl{B}")
                end = n == 2 and c == len(parts) - 1
                name = None
                if end and i < NT and k == B:
                    name = used(i)
                elif end and i == NT - 1:
                    name = f"k{i}.{k}"
                op("tensor", lambda e, x=x, w=w, c0=c0, c1=c1, bank=bank, n=n, end=end: e.matmul(
                    bank[:, 0:c1 - c0], xs(x, k), w[k][:, c0:c1], start=n == k == 0,
                    stop=end and k == B and h == 0), name, after)

    def low_pe(i):
        h, t = tiles[i]
        parts = chunks(i)
        for c, (c0, _, c1, bank) in enumerate(parts):
            apart = c == 2
            op("tensor", lambda e, c0=c0, c1=c1, dst=pm if apart else bank, apart=apart: e.matmul(
                dst[:, 0:c1 - c0], sa[t], bs[:, h * H + c0:h * H + c1], start=apart, stop=True),
                f"pt{i}" if c == len(parts) - 1 else None, [f"ml{t}", "bs"])

    def evacuate(i):
        free = [f"st{i - 2}"] if i >= 2 else ["sg.last", last_we]
        for c, (c0, _, c1, bank) in enumerate(chunks(i)):
            dst, src = os_[i % 2][:, c0:c1], bank[:, 0:c1 - c0]
            if c == 2:
                op("scalar", lambda e, dst=dst, src=src: e.activation(dst, src, ACT.Copy), f"oc{i}", [used(i), *free])
                op("vector", lambda e, dst=dst, c0=c0, c1=c1: e.tensor_tensor(dst, dst, pm[:, 0:c1 - c0], ALU.add),
                   f"o{i}.2", [f"pt{i}", f"oc{i}"])
            elif c == 1 and i >= NT:
                op("vector", lambda e, dst=dst, src=src: e.tensor_copy(dst, src), f"o{i}.1", [f"pt{i}", *free])
            else:
                op("scalar", lambda e, dst=dst, src=src: e.activation(dst, src, ACT.Copy), f"o{i}.{c}",
                   [f"pt{i}", *free])

    def store(i):
        h, t = tiles[i]
        dma("sync", f"st{i % 2}", out[t, :, h * H:(h + 1) * H], os_[i % 2], f"st{i}",
            [f"o{i}.{c}" for c in range(len(chunks(i)))])

    def hops_pe(i, k):
        for hop, at in zip((turn_pe, mix_pe, low_pe), (10, 12, 14) if i == NT - 1 else (3, 7, 10)):
            if k == at:
                hop(i)

    load_x(0)
    split(0)
    prepare_low()
    load_x(1)
    for k in range(B):
        load_g(0, k)
        if k < B - 1:
            split_g(0, k)
    finish_last()
    split_g(0, B - 1)
    for i in range(N):
        for k in range(NB):
            main_pe(i, k)
            if 1 <= i <= NT:
                hops_pe(i - 1, k)
        if i >= NT:
            low_pe(i)
        fresh = i + 1 < N and kept(i + 1) == i + 1
        if i and fresh:
            load_x(i + 1)
        if 1 <= i <= NT:
            if i < NT:
                route_chain(i - 1)
            turn_act(i - 1)
            if fresh:
                split(i + 1)
            mix_out(i - 1)
            if i == NT - 1:
                for k in range(NB):
                    load_g(1, k)
                    split_g(1, k)
                    if k == 5:
                        evacuate(i - 1)
                        store(i - 1)
                    if k == 11:
                        route_chain(i)
            else:
                evacuate(i - 1)
                store(i - 1)
        elif i == 0:
            split(1)
        else:
            evacuate(i - 1)
            store(i - 1)
            if fresh:
                split(i + 1)
    evacuate(N - 1)
    store(N - 1)
    pl.end("sync", [f"st{N - 2}", f"st{N - 1}"])


def build(nc, io, out):
    g_raw = nc.dram_tensor("g_raw", [NB, 128, D], F32, kind="Internal").ap()
    with ExitStack() as ctx:
        plan = Plan(nc, ctx)
        room = Room(nc, ctx)
        plan_weights(plan, room, io, g_raw)
        plan_tokens(plan, room, io, g_raw, out)
        run_block(nc, plan)


def kernel(x, condB_codebook, L0_cond_weight, L0_cond_scale_log, L0_cond_lora_A, L0_cond_lora_B, L0_ffn_W_base,
           L0_ffn_b_base, L0_ffn_A_w, L0_ffn_B_w, L0_ffn_router_w, L0_ffn_cores):
    import concourse.bacc as bacc
    from concourse.bass_utils import run_bass_kernel_spmd

    def lay(a):
        return np.ascontiguousarray(a)

    x = np.asarray(x)
    wide = np.concatenate([np.asarray(L0_ffn_W_base), np.asarray(L0_ffn_A_w), np.asarray(L0_ffn_router_w)], axis=0)
    la = np.asarray(L0_cond_lora_A)
    arrays = {
        "x": lay(x.reshape(NT, 128, NB, 128).transpose(0, 3, 2, 1).reshape(NT, 128, D)),
        "w": lay(np.asarray(L0_cond_weight).reshape(NB, 128, NB, 128).transpose(2, 1, 0, 3).reshape(NB, 128, D)),
        "sl": lay(np.asarray(L0_cond_scale_log).reshape(NB, 128, NB).transpose(1, 2, 0).reshape(128, NB * NB)),
        "lb": lay(np.asarray(L0_cond_lora_B).reshape(2, 1024, 64).transpose(0, 2, 1).reshape(128, 1024)),
        "la": lay(np.concatenate([la, la], axis=0)),
        "wb": lay(wide.T.reshape(NB, 128, DX)),
        "cores": lay(np.asarray(L0_ffn_cores).reshape(128, NR)),
        "bw": lay(np.asarray(L0_ffn_B_w).T),
        "b": lay(np.asarray(L0_ffn_b_base).reshape(1, D)),
        "cb": lay(np.asarray(condB_codebook)),
        "id": np.eye(128, dtype=np.float32),
    }
    nc = bacc.Bacc("TRN2", target_bir_lowering=False, num_devices=1)
    io = {k: nc.dram_tensor(f"in_{k}", a.shape, F32, kind="ExternalInput").ap() for k, a in arrays.items()}
    out = nc.dram_tensor("out", [NT, 128, D], F32, kind="ExternalOutput").ap()
    build(nc, io, out)
    r = run_bass_kernel_spmd(nc, [{f"in_{k}": a for k, a in arrays.items()}], core_ids=[0])
    return r.results[0]["out"].reshape(32, 128, D)
```
